# Optimizing a Trainium2 kernel written in Bass

```python
import numpy as np
import jax
import jax.numpy as jnp

def _softmax(x, axis=-1):
    return jax.nn.softmax(x, axis=axis)

def _gelu(x):
    return jax.nn.gelu(x, approximate=True)

def _silu(x):
    return jax.nn.silu(x)

def _sigmoid(x):
    return jax.nn.sigmoid(x)

def _layernorm(x, axis=-1, eps=1e-05):
    m = jnp.mean(x, axis=axis, keepdims=True)
    v = jnp.var(x, axis=axis, keepdims=True)
    return (x - m) / jnp.sqrt(v + eps)

def _scatter_add(tgt, idx, src, axis=0):
    return tgt.at[idx].add(src)

def _segment_sum(src, seg, n):
    return jax.ops.segment_sum(src, seg, n)
kernel_name = 'mk_adj_resnorm_d2_adj_r2_6a0649'

def setup_inputs(seed: int=0):
    np.random.seed(seed)
    _w = jnp.asarray

    def _rec_inputs():
        import jax
        import jax.numpy as jnp
        _gk = jax.random.key(seed)
        x = -0.0002928 + 1 * jax.random.normal(jax.random.fold_in(_gk, 1), (2048, 256), jnp.float32)
        _a = jax.random.bernoulli(jax.random.fold_in(_gk, 2), 0.000976562, (2048, 2048))
        _a = jnp.logical_or(_a, jnp.swapaxes(_a, -1, -2))
        _a = jnp.logical_or(_a, jnp.eye(2048, dtype=bool))
        _af = _a.astype(jnp.float32)
        _af = _af * jax.random.uniform(jax.random.fold_in(_gk, 3), (2048, 2048), jnp.float32, 0.05, 5.41998)
        adj = _af
        return (x, adj)
    x, adj = _rec_inputs()

    def _L0_gnn_setup():
        import jax, jax.numpy as jnp
        import numpy as np
        N = 4096
        D = 256
        EPS = 1e-12
        key = jax.random.key(seed)
        k1, k2 = jax.random.split(key)
        cur = jax.random.normal(k1, (N, D), dtype=jnp.float32)
        incidence_m = jax.random.normal(k2, (N, N), dtype=jnp.float32)
        return {'cur': cur, 'incidence_m': incidence_m}
    _L0_gnn_all = _L0_gnn_setup()
    _L0_gnn_in = {k: v for k, v in _L0_gnn_all.items() if k in ()}
    del _L0_gnn_all

    def _L1_gnn_setup():
        import jax, jax.numpy as jnp
        import numpy as np
        N = 3072
        D_IN = 256
        D_OUT = 256
        DENSITY = 0.005
        key = jax.random.key(seed)
        ks = jax.random.split(key, 12)
        x = jax.random.normal(ks[0], (N, D_IN), dtype=jnp.float32)
        adj_a = (jax.random.uniform(ks[1], (N, N)) < DENSITY).astype(jnp.float32)
        adj_b = (jax.random.uniform(ks[2], (N, N)) < DENSITY).astype(jnp.float32)
        W_sa = jax.random.normal(ks[3], (D_IN, D_OUT), dtype=jnp.float32) * (1.414 / np.sqrt(D_IN + D_OUT))
        a_sa = jax.random.normal(ks[4], (1, 2 * D_OUT), dtype=jnp.float32) * (1.414 / np.sqrt(1 + 2 * D_OUT))
        stdv = 1.0 / np.sqrt(D_OUT)
        W_gcnb = jax.random.uniform(ks[5], (D_IN, D_OUT), minval=-stdv, maxval=stdv, dtype=jnp.float32)
        b_gcnb = jax.random.uniform(ks[6], (D_OUT,), minval=-stdv, maxval=stdv, dtype=jnp.float32)
        s = 1.0 / np.sqrt(2 * D_IN)
        Wa = jax.random.uniform(ks[7], (1, 2 * D_IN), minval=-s, maxval=s, dtype=jnp.float32)
        ba = jax.random.uniform(ks[8], (1,), minval=-s, maxval=s, dtype=jnp.float32)
        Wb = jax.random.uniform(ks[9], (1, 2 * D_IN), minval=-s, maxval=s, dtype=jnp.float32)
        bb = jax.random.uniform(ks[10], (1,), minval=-s, maxval=s, dtype=jnp.float32)
        return {'x': x, 'adj_a': adj_a, 'adj_b': adj_b, 'W_sa': W_sa, 'a_sa': a_sa, 'W_gcnb': W_gcnb, 'b_gcnb': b_gcnb, 'Wa': Wa, 'ba': ba, 'Wb': Wb, 'bb': bb}
    _L1_gnn_all = _L1_gnn_setup()
    _L1_gnn_in = {k: v for k, v in _L1_gnn_all.items() if k in ('W_sa', 'a_sa', 'W_gcnb', 'b_gcnb', 'Wa', 'ba', 'Wb', 'bb')}
    del _L1_gnn_all
    return {'x': x, 'adj': adj, 'L1_gnn_W_sa': _L1_gnn_in['W_sa'], 'L1_gnn_a_sa': _L1_gnn_in['a_sa'], 'L1_gnn_W_gcnb': _L1_gnn_in['W_gcnb'], 'L1_gnn_b_gcnb': _L1_gnn_in['b_gcnb'], 'L1_gnn_Wa': _L1_gnn_in['Wa'], 'L1_gnn_ba': _L1_gnn_in['ba'], 'L1_gnn_Wb': _L1_gnn_in['Wb'], 'L1_gnn_bb': _L1_gnn_in['bb']}

def reference(x, adj, L1_gnn_W_sa, L1_gnn_a_sa, L1_gnn_W_gcnb, L1_gnn_b_gcnb, L1_gnn_Wa, L1_gnn_ba, L1_gnn_Wb, L1_gnn_bb):
    import jax
    import jax.numpy as jnp

    def _L0_gnn_ref(cur, incidence_m):
        import jax, jax.numpy as jnp
        import numpy as np
        N = 4096
        D = 256
        EPS = 1e-12
        mask = incidence_m > 0
        head = jax.lax.stop_gradient(mask.astype(incidence_m.dtype))
        head = head / jnp.maximum(jnp.sqrt(jnp.sum(head * head, axis=-1, keepdims=True)), EPS)
        inc = incidence_m + head
        edge_fea = inc @ cur
        edge_degree = jnp.sum(inc, axis=-1, keepdims=True)
        return edge_fea / edge_degree

    def _L1_gnn_ref(x, adj_a, adj_b, W_sa, a_sa, W_gcnb, b_gcnb, Wa, ba, Wb, bb):
        import jax, jax.numpy as jnp
        import numpy as np
        N = 3072
        D_IN = 256
        D_OUT = 256
        DENSITY = 0.005
        type_sum_a = adj_a @ x
        type_sum_b = adj_b @ x
        attn_a = jax.nn.sigmoid(jnp.concatenate([type_sum_a, x], axis=1) @ Wa.T + ba)
        attn_b = jax.nn.sigmoid(jnp.concatenate([type_sum_b, x], axis=1) @ Wb.T + bb)
        h = x @ W_sa
        Hd = h.shape[1]
        s_left = h @ a_sa[0, :Hd]
        s_right = h @ a_sa[0, Hd:]
        scores = s_left[:, None] + s_right[None, :]
        e = jnp.where(adj_a != 0, jnp.exp(-jax.nn.leaky_relu(scores, 0.01)), 0.0)
        attn = e / (jnp.sum(e, axis=1, keepdims=True) + 1e-05)
        x_a = attn @ h
        x_b = adj_b @ (x @ W_gcnb) + b_gcnb
        return jax.nn.sigmoid(attn_a * x_a + attn_b * x_b)
    x = _layernorm(x + _L0_gnn_ref(x, adj), axis=-1)
    x = _layernorm(x + _L1_gnn_ref(x, adj, adj, L1_gnn_W_sa, L1_gnn_a_sa, L1_gnn_W_gcnb, L1_gnn_b_gcnb, L1_gnn_Wa, L1_gnn_ba, L1_gnn_Wb, L1_gnn_bb), axis=-1)
    return x

_drawn_inputs = setup_inputs


def setup_inputs(seed=0):
    import zlib

    import numpy as np

    out = dict(_drawn_inputs(seed))
    spreads = {}
    factors = {'L1_gnn_a_sa': 2.986, 'L1_gnn_b_gcnb': 8.0}
    for name, (base, spread) in spreads.items():
        noise = np.random.default_rng([zlib.crc32(name.encode()), seed]).standard_normal(out[name].shape)
        drawn = base * np.exp(spread * noise) if base else spread * noise
        out[name] = jnp.asarray(drawn.astype(out[name].dtype))
    for name, factor in factors.items():
        out[name] = (out[name] * factor).astype(out[name].dtype)
    return out
```

```python
import concourse.bass as bass
from concourse import mybir
from contextlib import ExitStack

P = 128


def two_layer_gnn(nc, x, adj, adj_t, w_cat, a_sa, bias_row, out):
    F32, F32R, I8 = mybir.dt.float32, mybir.dt.float32r, mybir.dt.int8
    ALU, ACT, AX = mybir.AluOpType, mybir.ActivationFunctionType, mybir.AxisListType

    N, D = x.shape
    NB = N // P
    NQ = 4
    QT = NB // NQ
    QC = QT * P
    HALF = N // 2
    KT = D // P
    HC = D + 4
    GC = D + 2
    WC = HC + GC
    LN_EPS, COUNT_EPS, SUM_EPS, SLOPE = 1e-5, 1e-24, 1e-5, 0.01

    ctx = ExitStack()
    with ctx:
        def sb(name, shape, dt, stack=None):
            return (stack or ctx).enter_context(nc.sbuf_tensor(name, shape, dt))

        def bank(name):
            return ctx.enter_context(nc.psum_tensor(name, [P, 512], F32))

        def sem(name):
            return ctx.enter_context(nc.semaphore(name))

        h_hi, h_lo = sb("h_hi", [P, NB, D], F32R), sb("h_lo", [P, NB, D], F32R)
        g_hi, g_lo = sb("g_hi", [P, NB, GC], F32R), sb("g_lo", [P, NB, GC], F32R)
        x1 = sb("x1", [P, NB, D], F32)
        right = sb("right", [P, N], F32)
        blk_hi, blk_lo = sb("blk_hi", [P, NB, P], F32R), sb("blk_lo", [P, NB, P], F32R)
        rows = sb("rows", [P, 2, N], F32)
        cols = sb("cols", [P, 2, N], F32)
        w_f = sb("w_f", [P, KT, WC], F32)
        w_hi, w_lo = sb("w_hi", [P, KT, WC], F32R), sb("w_lo", [P, KT, WC], F32R)
        wide = sb("wide", [P, P], F32)
        xt_hi, xt_lo = sb("xt_hi", [P, KT, P], F32R), sb("xt_lo", [P, KT, P], F32R)
        brow = sb("brow", [P, GC], F32)
        brow_hi, brow_lo = sb("brow_hi", [P, GC], F32R), sb("brow_lo", [P, GC], F32R)
        first_row = sb("first_row", [P, P], F32R)
        ident = sb("ident", [P, P], F32)
        nodecols = sb("nodecols", [P, NB, 3], F32)
        left99, left01 = sb("left99", [P, NB], F32), sb("left01", [P, NB], F32)
        minus_half = sb("minus_half", [P, 1], F32)
        cnt = sb("cnt", [P, 1], F32)
        cnt_g = sb("cnt_g", [P, 1], F32)
        scale = sb("scale", [P, 1], F32)
        deg2 = sb("deg2", [P, 2], F32)
        deg = sb("deg", [P, 1], F32)
        rdeg = sb("rdeg", [P, 2], F32)
        stats, mv = sb("stats", [P, 6], F32), sb("mv", [P, 2], F32)
        var_g, rstd = sb("var_g", [P, 1], F32), sb("rstd", [P, 1], F32)
        y = sb("y", [P, D], F32)
        x1_now = sb("x1_now", [P, D], F32)
        one = ExitStack()
        a_bc = sb("a_bc", [P, 2 * D], F32)
        x_hi, x_lo = sb("x_hi", [P, NB, D], F32R, one), sb("x_lo", [P, NB, D], F32R, one)
        inc = sb("inc", [P, N], F32, one)
        sgn, pos = sb("sgn", [P, N], I8, one), sb("pos", [P, N], I8, one)
        one.close()
        ct_hi, ct_lo = sb("ct_hi", [P, NB, P], F32R), sb("ct_lo", [P, NB, P], F32R)
        e = sb("e", [P, 2, N], F32)
        right01 = sb("right01", [P, N], F32)
        rowsum4 = sb("rowsum4", [P, 2, NQ], F32)
        rowsum, rrow = sb("rowsum", [P, 1], F32), sb("rrow", [P, 1], F32)
        zl, tl, attn = sb("zl", [P, 2], F32), sb("tl", [P, 2], F32), sb("attn", [P, 2], F32)
        coef = sb("coef", [P, 1], F32)
        nb_part = sb("nb_part", [P, D], F32)
        z, th, sig = sb("z", [P, D], F32), sb("th", [P, D], F32), sb("sig", [P, D], F32)
        out_sb = sb("out_sb", [P, 2, D], F32)

        turned = [bank("turned0"), bank("turned1")]
        acc = [bank("acc0"), bank("acc1")]
        ps_x, ps_h, ps_g, ps_r = bank("ps_x"), bank("ps_h"), bank("ps_g"), bank("ps_r")

        rows_in = sem("rows_in")
        rows2_in = sem("rows2_in")
        cols_in = sem("cols_in")
        x_in = [sem(f"x_in{q}") for q in range(NQ)]
        w_in, a_in, b_in = sem("w_in"), sem("a_in"), sem("b_in")
        id0, id1, ones0, ones1 = sem("id0"), sem("id1"), sem("ones0"), sem("ones1")
        half_set, brow0 = sem("half_set"), sem("brow0")
        xhi_done, xlo_done = sem("xhi_done"), sem("xlo_done")
        sgn_done, cnt_done = sem("sgn_done"), sem("cnt_done")
        cntg_done, scale_done = sem("cntg_done"), sem("scale_done")
        inc_done = sem("inc_done")
        deg_done, rdeg_done = sem("deg_done"), sem("rdeg_done")
        turn_done = sem("turn_done")
        hi_done, lo_done = sem("hi_done"), sem("lo_done")
        acc_done, y_done = sem("acc_done"), sem("y_done")
        st_done, mv_done = sem("st_done"), sem("mv_done")
        varg_done, rstd_done = sem("varg_done"), sem("rstd_done")
        x1n_done, x1_kept = sem("x1n_done"), sem("x1_kept")
        xt_done, xthi_done, xtlo_done = sem("xt_done"), sem("xthi_done"), sem("xtlo_done")
        h_done, g_done, r_done = sem("h_done"), sem("g_done"), sem("r_done")
        hhi_done, hlo_done = sem("hhi_done"), sem("hlo_done")
        ghi_done, glo_done = sem("ghi_done"), sem("glo_done")
        right_done, nodecols_done = sem("right_done"), sem("nodecols_done")
        v_done, whi_done, wlo_done, wide_done = sem("v_done"), sem("whi_done"), sem("wlo_done"), sem("wide_done")
        bhi_done, blo_done = sem("bhi_done"), sem("blo_done")
        left_done, right01_done = sem("left_done"), sem("right01_done")
        arg_done, exp_done, mask_done = sem("arg_done"), sem("exp_done"), sem("mask_done")
        cthi_done, ctlo_done, ctq_used = sem("cthi_done"), sem("ctlo_done"), sem("ctq_used")
        ag_done, eh_done = sem("ag_done"), sem("eh_done")
        zl_done, tl_done, attn_done = sem("zl_done"), sem("tl_done"), sem("attn_done")
        rs_done, rse_done, rrow_done, coef_done = (
            sem("rs_done"), sem("rse_done"), sem("rrow_done"), sem("coef_done"))
        nbp_done, z_done, th_done, sig_done = sem("nbp_done"), sem("z_done"), sem("th_done"), sem("sig_done")
        y2_done, out_done, out_stored = sem("y2_done"), sem("out_done"), sem("out_stored")

        sp_waits, act_waits, pool_waits, dve_waits = sem("sp_waits"), sem("act_waits"), sem("pool_waits"), sem("dve_waits")

        block = ctx.enter_context(nc.Block())

        def once(eng, s, value):
            if not isinstance(value, int) or value > 0:
                eng.wait_ge(s, value)

        def steps(eng, step, first, last):
            lo, hi = 2, NB - 2

            def has(b):
                return {k: 0 <= b - k < NB for k in range(-2, 3)}
            for b in range(first, lo):
                step(b, b % 2, has(b))
            with eng.Fori(lo // 2, hi // 2) as t:
                for s in range(2):
                    step(2 * t + s, s, has(lo))
            for b in range(hi, last + 1):
                step(b, b % 2, has(b))

        def steps2(eng, step):
            step(0, 0, True, False)
            step(1, 1, False, False)
            with eng.Fori(1, NB // 2 - 1) as t:
                for s in range(2):
                    step(2 * t + s, s, False, False)
            step(NB - 2, 0, False, False)
            step(NB - 1, 1, False, True)

        def quarter(t, q):
            return t[:, q * QC:(q + 1) * QC]

        def tiles(t, q):
            return t[:, q * QT:(q + 1) * QT, :].rearrange("p t c -> p (t c)")

        @block.sync
        def _(sp):
            adj_b = adj.rearrange("(b p) n -> b p n", p=P)
            x_v = x.rearrange("(t p) d -> p t d", p=P)
            out_b = out.rearrange("(b p) d -> b p d", p=P)
            def load_x(q):
                sp.dma_start(x1[:, q * QT:(q + 1) * QT, :], x_v[:, q * QT:(q + 1) * QT, :]).then_inc(x_in[q], 16)

            sp.dma_start(rows[:, 0, :], adj_b[0]).then_inc(rows_in, 16)
            load_x(0)
            sp.wait_ge(rows_in, 16)
            sp.dma_start(rows[:, 1, :], adj_b[1]).then_inc(rows_in, 16)
            for q in range(1, NQ):
                load_x(q)
            sp.dma_start(w_f[:, :, :], w_cat.rearrange("(k p) c -> p k c", p=P)).then_inc(w_in, 16)
            sp.dma_start(a_bc[:, :], a_sa.partition_broadcast(P)).then_inc(a_in, 16)
            sp.wait_ge(brow0, 1)
            sp.dma_start(brow[0:1, :], bias_row).then_inc(b_in, 16)
            with sp.Fori(1, NB // 2) as t:
                for s in range(2):
                    b = 2 * t + s
                    sp.wait_ge(rows_in, 16 * b)
                    sp.sem_inc(sp_waits, 1)
                    sp.wait_ge(inc_done, 2 * (b - 2) + 2)
                    sp.sem_inc(sp_waits, 1)
                    sp.dma_start(rows[:, s, :], adj_b[b]).then_inc(rows_in, 16)
            for b in range(2):
                if b:
                    sp.wait_ge(cols_in, 16)
                    sp.wait_ge(rows2_in, 16)
                sp.dma_start(cols[:, b, :], adj_t[b]).then_inc(cols_in, 16)
                sp.wait_ge(inc_done, 2 * (NB - 2 + b) + 2)
                sp.dma_start(rows[:, b, :], adj_b[b]).then_inc(rows2_in, 16)

            def load(b, s):
                sp.wait_ge(rows2_in, 16 * b)
                sp.sem_inc(sp_waits, 1)
                sp.wait_ge(mask_done, NQ * (b - 2) + NQ)
                sp.sem_inc(sp_waits, 1)
                sp.dma_start(rows[:, s, :], adj_b[b]).then_inc(rows2_in, 16)
                sp.wait_ge(cols_in, 16 * b)
                sp.sem_inc(sp_waits, 1)
                sp.wait_ge(ctlo_done, NQ * (b - 2) + NQ)
                sp.sem_inc(sp_waits, 1)
                sp.dma_start(cols[:, s, :], adj_t[b]).then_inc(cols_in, 16)

            def store(b, s, first=False):
                if not first:
                    sp.wait_ge(out_stored, 16 * b)
                    sp.sem_inc(sp_waits, 1)
                sp.wait_ge(out_done, b + 1)
                sp.sem_inc(sp_waits, 1)
                sp.dma_start(out_b[b], out_sb[:, s, :]).then_inc(out_stored, 16)

            LAG = 4
            for b in range(2, LAG + 2):
                load(b, b % 2)
                if b >= LAG:
                    store(b - LAG, b % 2, first=b == LAG)
            with sp.Fori(LAG // 2 + 1, NB // 2) as t:
                for s in range(2):
                    load(2 * t + s, s)
                    store(2 * t + s - LAG, s)
            for b in range(NB - LAG, NB):
                store(b, b % 2)
            sp.wait_ge(out_stored, 16 * NB)

        @block.gpsimd
        def _(pool):
            pool.memset(ident[:, :], 0.0).then_inc(id0, 1)
            pool.memset(minus_half[:, :], -0.5).then_inc(half_set, 1)
            pool.memset(first_row[:, :].bitcast(F32), 0.0).then_inc(ones0, 1)
            pool.memset(brow[:, :], 0.0).then_inc(brow0, 1)
            pool.wait_ge(id0, 1)
            pool.affine_select(out=ident[:, :], in_=ident[:, :], compare_op=ALU.not_equal, fill=1.0, base=0,
                               pattern=[[-1, P]], channel_multiplier=1).then_inc(id1, 1)
            pool.wait_ge(ones0, 1)
            pool.memset(first_row[0:1, :].bitcast(F32), 1.0).then_inc(ones1, 1)
            pool.wait_ge(half_set, 1)

            def rsqrt_of_var(n, n_first):
                once(pool, rstd_done, n)
                pool.wait_ge(mv_done, n + 1)
                pool.sem_inc(pool_waits, 1)
                pool.tensor_scalar(var_g[:, :], mv[:, 1:2], LN_EPS, 1.0, ALU.add, ALU.mult).then_inc(varg_done, 1)
                pool.wait_ge(varg_done, n + 1)
                once(pool, x1n_done, n if n_first else NB)
                if not n_first:
                    once(pool, out_done, n - NB)
                pool.tensor_tensor(rstd[:, :], var_g[:, :], minus_half[:, :], ALU.pow).then_inc(rstd_done, 1)

            def step(b, s, has):
                if has[1]:
                    rsqrt_of_var(b - 1, True)
                if has[-2]:
                    once(pool, scale_done, b + 2)
                    pool.wait_ge(cnt_done, b + 3)
                    pool.sem_inc(pool_waits, 1)
                    pool.tensor_scalar(cnt_g[:, :], cnt[:, :], float(2 * N), COUNT_EPS, ALU.min, ALU.max).then_inc(cntg_done, 1)
                    pool.wait_ge(cntg_done, b + 3)
                    once(pool, inc_done, 2 * (b + 1) + 2 if not isinstance(b, int) or b > -2 else 0)
                    pool.tensor_tensor(scale[:, :], cnt_g[:, :], minus_half[:, :], ALU.pow).then_inc(scale_done, 1)
                if has[1]:
                    pool.wait_ge(x1n_done, b)
                    pool.sem_inc(pool_waits, 1)
                    pool.tensor_copy(x1[:, b - 1, :], x1_now[:, :]).then_inc(x1_kept, 1)

            steps(pool, step, -2, NB)

            def final(b):
                once(pool, y2_done, b)
                pool.wait_ge(th_done, b + 1)
                pool.sem_inc(pool_waits, 1)
                pool.tensor_scalar(sig[:, :], th[:, :], 0.5, 0.5, ALU.mult, ALU.add).then_inc(sig_done, 1)
                pool.wait_ge(sig_done, b + 1)
                once(pool, out_done, b)
                pool.sem_inc(pool_waits, 1)
                pool.tensor_tensor(y[:, :], x1[:, b, :], sig[:, :], ALU.add).then_inc(y2_done, 1)
                rsqrt_of_var(NB + b, False)

            final(0)
            with pool.Fori(1, NB) as b:
                final(b)

        @block.scalar
        def _(act):
            def split_hi(n, q):
                act.wait_ge(turn_done, n + 1)
                nc.scalar.copy(tiles(blk_hi, q), turned[q % 2][:, :]).then_inc(hi_done, 1)

            def signs(b, s):
                act.wait_ge(rows_in, 16 * (b + 1))
                once(act, cnt_done, b)
                nc.scalar.activation(sgn[:, :], rows[:, s, :], ACT.Sign).then_inc(sgn_done, 1)

            def positives(b):
                act.wait_ge(sgn_done, b)
                act.wait_ge(inc_done, 2 * b)
                act.wait_ge(cntg_done, b)
                nc.scalar.activation(pos[:, :], sgn[:, :], ACT.Relu, accum_out=cnt[:, :]).then_inc(cnt_done, 1)

            def x_to_hi(q):
                act.wait_ge(x_in[q], 16)
                nc.scalar.copy(x_hi[:, q * QT:(q + 1) * QT, :], x1[:, q * QT:(q + 1) * QT, :]).then_inc(xhi_done, 1)

            def step(b, s, has):
                if isinstance(b, int) and b == -2:
                    x_to_hi(0)
                    return
                if isinstance(b, int) and b == -1:
                    signs(1, 1)
                for q in range(NQ):
                    if has[2] and q == 0:
                        act.wait_ge(xt_done, b - 1)
                        nc.scalar.copy(xt_hi[:, :, :].rearrange("p k c -> p (k c)"), ps_x[:, 0:D]).then_inc(xthi_done, 1)
                    if has[-1]:
                        split_hi(NQ * (b + 1) + q, q)
                    if has[-2] and q == 0 and not (isinstance(b, int) and b == -1):
                        signs(b + 2, s)
                    if isinstance(b, int) and b == -1 and q > 0:
                        x_to_hi(q)
                    if has[-2] and q == 1:
                        positives(b + 2)
                    if has[2] and q == 2:
                        act.wait_ge(h_done, b - 1)
                        once(act, r_done, b - 2)
                        nc.scalar.copy(wide[:, :], ps_h[:, D + 3:D + 4].to_broadcast([P, P])).then_inc(wide_done, 1)
                        nc.scalar.copy(h_hi[:, b - 2, :], ps_h[:, 0:D]).then_inc(hhi_done, 1)
                    if has[2] and q == 3:
                        act.wait_ge(g_done, b - 1)
                        act.sem_inc(act_waits, 1)
                        nc.scalar.copy(g_hi[:, b - 2, :], ps_g[:, 0:GC]).then_inc(ghi_done, 1)
                        act.wait_ge(r_done, b - 1)
                        act.sem_inc(act_waits, 1)
                        nc.scalar.copy(right[:, bass.ts(b - 2, P)], ps_r[:, 0:P]).then_inc(right_done, 1)
                if isinstance(b, int) and b == 0:
                    act.wait_ge(v_done, 2 * KT)
                    nc.scalar.copy(w_hi[:, :, :], w_f[:, :, :]).then_inc(whi_done, 1)
                    act.wait_ge(b_in, 16)
                    nc.scalar.copy(brow_hi[:, :], brow[:, :]).then_inc(bhi_done, 1)

            steps(act, step, -2, NB + 1)

            def exps(b, s, q):
                act.wait_ge(arg_done, NQ * b + q + 1)
                if q == 0:
                    act.wait_ge(left_done, 2)
                act.sem_inc(act_waits, 1)
                eq = quarter(e[:, s, :], q)
                nc.scalar.activation(eq, eq, ACT.Exp, bias=left01[:, bass.ds(b, 1)], scale=-1.0).then_inc(exp_done, 1)

            def cols_hi(b, s, q):
                if q == 0:
                    act.wait_ge(cols_in, 16 * (b + 1))
                once(act, ctq_used, NQ * (b - 1) + q + 1)
                nc.scalar.copy(tiles(ct_hi, q), quarter(cols[:, s, :], q)).then_inc(cthi_done, 1)

            def gates(b):
                once(act, attn_done, b)
                act.wait_ge(zl_done, b + 1)
                nc.scalar.activation(tl[:, :], zl[:, :], ACT.Tanh, scale=0.5).then_inc(tl_done, 1)

            def neighbours(b):
                once(act, z_done, b)
                act.wait_ge(attn_done, b + 1)
                nc.scalar.activation(nb_part[:, :], acc[1][:, 0:D], ACT.Copy, scale=attn[:, 1:2]).then_inc(nbp_done, 1)

            def final(b):
                once(act, sig_done, b)
                act.wait_ge(z_done, b + 1)
                nc.scalar.activation(th[:, :], z[:, :], ACT.Tanh, scale=0.5).then_inc(th_done, 1)

            for q in range(NQ):
                cols_hi(0, 0, q)
                exps(0, 0, q)

            def step2(b, s, first, last):
                for q in range(NQ):
                    if q > 0 and not last:
                        exps(b + 1, 1 - s, q - 1)
                    split_hi(NQ * NB + NQ * b + q, q)
                    if q == 0 and not first:
                        final(b - 1)
                if last:
                    gates(b)
                    neighbours(b)
                else:
                    cols_hi(b + 1, 1 - s, 0)
                    gates(b)
                    exps(b + 1, 1 - s, NQ - 1)
                    cols_hi(b + 1, 1 - s, 1)
                    neighbours(b)
                    cols_hi(b + 1, 1 - s, 2)
                    cols_hi(b + 1, 1 - s, 3)

            steps2(act, step2)
            final(NB - 1)

        @block.vector
        def _(dve):
            def split_lo(n, q):
                dve.wait_ge(hi_done, n + 1)
                nc.vector.tensor_tensor(tiles(blk_lo, q), turned[q % 2][:, :], tiles(blk_hi, q).bitcast(F32),
                                        ALU.subtract).then_inc(lo_done, 1)

            def build_inc(b, s, half):
                if half == 0:
                    dve.wait_ge(scale_done, b + 1)
                if not isinstance(b, int) or b > 0:
                    dve.wait_ge(turn_done, NQ * (b - 1) + 2 * half + 2)
                    if half == 0:
                        dve.wait_ge(deg_done, b)
                c = slice(half * HALF, (half + 1) * HALF)
                nc.vector.scalar_tensor_tensor(out=inc[:, c], in0=pos[:, c], scalar=scale[:, :], in1=rows[:, s, c],
                                               op0=ALU.mult, op1=ALU.add, accum_out=deg2[:, half:half + 1]).then_inc(inc_done, 1)

            def layer_norm_stats(n):
                once(dve, varg_done, n)
                once(dve, mv_done, n)
                nc.vector.bn_stats(stats[:, :], y[:, :]).then_inc(st_done, 1)
                dve.wait_ge(st_done, n + 1)
                dve.sem_inc(dve_waits, 1)
                nc.vector.bn_aggr(mv[:, :], stats[:, :]).then_inc(mv_done, 1)

            def x_to_lo(q):
                dve.wait_ge(xhi_done, q + 1)
                t = slice(q * QT, (q + 1) * QT)
                nc.vector.tensor_tensor(x_lo[:, t, :], x1[:, t, :], x_hi[:, t, :].bitcast(F32),
                                        ALU.subtract).then_inc(xlo_done, 1)

            def step(b, s, has):
                if isinstance(b, int) and b == -2:
                    dve.wait_ge(rows_in, 16)
                    nc.vector.tensor_scalar(pos[:, :], rows[:, 0, :], 0.0, None, ALU.is_gt, ALU.add,
                                            accum_out=cnt[:, :]).then_inc(cnt_done, 1)
                if has[1]:
                    once(dve, x1n_done, b - 1)
                    dve.wait_ge(rdeg_done, b)
                    dve.wait_ge(acc_done, b)
                    nc.vector.scalar_tensor_tensor(out=y[:, :], in0=acc[1 - s][:, 0:D], scalar=rdeg[:, 1 - s:2 - s],
                                                   in1=x1[:, b - 1, :], op0=ALU.mult, op1=ALU.add).then_inc(y_done, 1)
                if has[2]:
                    dve.wait_ge(xthi_done, b - 1)
                    nc.vector.tensor_tensor(xt_lo[:, :, :].rearrange("p k c -> p (k c)"), ps_x[:, 0:D],
                                            xt_hi[:, :, :].rearrange("p k c -> p (k c)").bitcast(F32),
                                            ALU.subtract).then_inc(xtlo_done, 1)
                if has[1]:
                    dve.wait_ge(y_done, b)
                    layer_norm_stats(b - 1)
                if has[-1]:
                    build_inc(b + 1, 1 - s, 1)
                if has[-1]:
                    split_lo(NQ * (b + 1), 0)
                    dve.wait_ge(inc_done, 2 * (b + 1) + 2)
                    once(dve, rdeg_done, b + 1)
                    nc.vector.tensor_tensor(deg[:, :], deg2[:, 0:1], deg2[:, 1:2], ALU.add).then_inc(deg_done, 1)
                if has[-1]:
                    once(dve, y_done, b)
                    dve.wait_ge(deg_done, b + 2)
                    nc.vector.reciprocal(rdeg[:, 1 - s:2 - s], deg[:, :]).then_inc(rdeg_done, 1)
                    split_lo(NQ * (b + 1) + 1, 1)
                if isinstance(b, int) and b == -1:
                    x_to_lo(1)
                if has[1]:
                    dve.wait_ge(rstd_done, b)
                    once(dve, xt_done, b - 1)
                    once(dve, x1_kept, b - 1)
                    nc.vector.tensor_scalar(x1_now[:, :], y[:, :], mv[:, 0:1], rstd[:, :], ALU.subtract,
                                            ALU.mult).then_inc(x1n_done, 1)
                if has[-1]:
                    split_lo(NQ * (b + 1) + 2, 2)
                if has[-2]:
                    build_inc(b + 2, s, 0)
                if has[2]:
                    dve.wait_ge(hhi_done, b - 1)
                    nc.vector.tensor_copy(nodecols[:, b - 2, :], ps_h[:, D:D + 3]).then_inc(nodecols_done, 1)
                    nc.vector.tensor_tensor(h_lo[:, b - 2, :], ps_h[:, 0:D], h_hi[:, b - 2, :].bitcast(F32),
                                            ALU.subtract).then_inc(hlo_done, 1)
                if has[-1]:
                    split_lo(NQ * (b + 1) + 3, 3)
                if has[2]:
                    dve.wait_ge(ghi_done, b - 1)
                    nc.vector.tensor_tensor(g_lo[:, b - 2, :], ps_g[:, 0:GC], g_hi[:, b - 2, :].bitcast(F32),
                                            ALU.subtract).then_inc(glo_done, 1)
                if isinstance(b, int) and b == -2:
                    x_to_lo(0)
                if isinstance(b, int) and b == -1:
                    x_to_lo(2)
                    x_to_lo(3)
                    dve.wait_ge(w_in, 16)
                    dve.wait_ge(a_in, 16)
                    for k in range(KT):
                        for i, to in enumerate((w_f[:, k, D:D + 1], w_f[:, k, D + 3:D + 4])):
                            n = 2 * k + i
                            once(dve, v_done, n)
                            nc.vector.scalar_tensor_tensor(out=products, in0=w_f[:, k, 0:D], scalar=1.0,
                                                           in1=a_bc[:, i * D:(i + 1) * D], op0=ALU.mult, op1=ALU.mult,
                                                           accum_out=to).then_inc(v_done, 1)
                if isinstance(b, int) and b == 1:
                    dve.wait_ge(whi_done, 1)
                    nc.vector.tensor_tensor(w_lo[:, :, :], w_f[:, :, :], w_hi[:, :, :].bitcast(F32),
                                            ALU.subtract).then_inc(wlo_done, 1)
                    dve.wait_ge(bhi_done, 1)
                    nc.vector.tensor_tensor(brow_lo[:, :], brow[:, :], brow_hi[:, :].bitcast(F32),
                                            ALU.subtract).then_inc(blo_done, 1)

            products = h_lo[:, 0, :]
            steps(dve, step, -2, NB + 1)

            def arg(b, s, q):
                if not isinstance(b, int) or b > 1:
                    dve.wait_ge(turn_done, NQ * NB + NQ * (b - 2) + q + 1)
                nc.vector.scalar_tensor_tensor(out=quarter(e[:, s, :], q), in0=quarter(right, q),
                                               scalar=left99[:, bass.ds(b, 1)], in1=quarter(right01, q),
                                               op0=ALU.add, op1=ALU.max).then_inc(arg_done, 1)

            def mask(b, s, q):
                dve.wait_ge(exp_done, NQ * b + q + 1)
                if q == 0:
                    dve.wait_ge(rows2_in, 16 * (b + 1))
                    if not isinstance(b, int) or b > 1:
                        dve.wait_ge(rs_done, b - 1)
                eq = quarter(e[:, s, :], q)
                nc.vector.scalar_tensor_tensor(out=eq, in0=quarter(rows[:, s, :], q), scalar=0.0, in1=eq,
                                               op0=ALU.not_equal, op1=ALU.mult,
                                               accum_out=rowsum4[:, s, q:q + 1]).then_inc(mask_done, 1)

            def cols_lo(b, s, q):
                dve.wait_ge(cthi_done, NQ * b + q + 1)
                nc.vector.tensor_tensor(tiles(ct_lo, q), quarter(cols[:, s, :], q), tiles(ct_hi, q).bitcast(F32),
                                        ALU.subtract).then_inc(ctlo_done, 1)

            def logits(b):
                once(dve, tl_done, b)
                dve.wait_ge(ag_done, b + 1)
                nc.vector.tensor_tensor(zl[:, :], acc[1][:, D:D + 2], nodecols[:, b, 1:3], ALU.add).then_inc(zl_done, 1)

            def rowsums(b, s):
                dve.wait_ge(mask_done, NQ * b + NQ)
                once(dve, rse_done, b)
                nc.vector.reduce_sum(rowsum[:, :], rowsum4[:, s, :], axis=AX.X).then_inc(rs_done, 1)

            def coefficients(b):
                once(dve, coef_done, b)
                once(dve, nbp_done, b)
                dve.wait_ge(tl_done, b + 1)
                nc.vector.tensor_scalar(attn[:, :], tl[:, :], 0.5, 0.5, ALU.mult, ALU.add).then_inc(attn_done, 1)
                dve.wait_ge(rs_done, b + 1)
                nc.vector.tensor_scalar(rrow[:, :], rowsum[:, :], SUM_EPS, None, ALU.add).then_inc(rse_done, 1)
                dve.wait_ge(rse_done, b + 1)
                nc.vector.reciprocal(rrow[:, :], rrow[:, :]).then_inc(rrow_done, 1)
                dve.wait_ge(rrow_done, b + 1)
                dve.wait_ge(attn_done, b + 1)
                once(dve, z_done, b)
                nc.vector.tensor_tensor(coef[:, :], rrow[:, :], attn[:, 0:1], ALU.mult).then_inc(coef_done, 1)

            def combine(b):
                once(dve, th_done, b)
                dve.wait_ge(eh_done, b + 1)
                dve.wait_ge(nbp_done, b + 1)
                dve.wait_ge(coef_done, b + 1)
                nc.vector.scalar_tensor_tensor(out=z[:, :], in0=acc[0][:, 0:D], scalar=coef[:, :], in1=nb_part[:, :],
                                               op0=ALU.mult, op1=ALU.add).then_inc(z_done, 1)

            def stats2(b):
                dve.wait_ge(y2_done, b + 1)
                layer_norm_stats(NB + b)

            def finish(b, s):
                dve.wait_ge(rstd_done, NB + b + 1)
                if not isinstance(b, int) or b > 1:
                    dve.wait_ge(out_stored, 16 * (b - 1))
                nc.vector.tensor_scalar(out_sb[:, s, :], y[:, :], mv[:, 0:1], rstd[:, :], ALU.subtract,
                                        ALU.mult).then_inc(out_done, 1)

            dve.wait_ge(nodecols_done, NB)
            nc.vector.tensor_scalar(left99[:, :], nodecols[:, :, 0], 1.0 - SLOPE, None, ALU.mult).then_inc(left_done, 1)
            nc.vector.tensor_scalar(left01[:, :], nodecols[:, :, 0], -SLOPE, None, ALU.mult).then_inc(left_done, 1)
            dve.wait_ge(left_done, 2)
            for q in range(NQ):
                dve.wait_ge(right_done, QT * (q + 1))
                nc.vector.tensor_scalar(quarter(right01, q), quarter(right, q), SLOPE, None, ALU.mult).then_inc(right01_done, 1)
                cols_lo(0, 0, q)
                dve.wait_ge(right01_done, q + 1)
                arg(0, 0, q)
            for q in range(NQ):
                mask(0, 0, q)

            def step2(b, s, first, last):
                nxt, s1 = b + 1, 1 - s
                for q in range(NQ):
                    if not last:
                        arg(nxt, s1, q)
                        if q == 3:
                            mask(nxt, s1, 1)
                    if q == 0 and not first:
                        combine(b - 1)
                    split_lo(NQ * NB + NQ * b + q, q)
                    if q == 1 and not last:
                        mask(nxt, s1, 0)
                    if q == 2 and not first:
                        stats2(b - 1)
                logits(b)
                rowsums(b, s)
                if not last:
                    cols_lo(nxt, s1, 0)
                coefficients(b)
                if not first:
                    finish(b - 1, s1)
                if not last:
                    cols_lo(nxt, s1, 1)
                    mask(nxt, s1, 2)
                    cols_lo(nxt, s1, 2)
                    mask(nxt, s1, 3)
                    cols_lo(nxt, s1, 3)

            steps2(dve, step2)
            combine(NB - 1)
            stats2(NB - 1)
            finish(NB - 1, (NB - 1) % 2)

        @block.tensor
        def _(pe):
            def transpose_quarter(n, src, q):
                if not isinstance(n, int) or n >= 2:
                    pe.wait_ge(lo_done, n - 1)
                for t in range(QT):
                    last = nc.tensor.transpose(turned[q % 2][:, t * P:(t + 1) * P],
                                               src[:, (q * QT + t) * P:(q * QT + t + 1) * P], ident[:, :])
                last.then_inc(turn_done, 1)

            def three(dst, hi, lo, mv_hi, mv_lo, start, stop):
                nc.tensor.matmul(dst, hi, mv_hi, start=start, stop=False)
                nc.tensor.matmul(dst, hi, mv_lo, start=False, stop=False)
                return nc.tensor.matmul(dst, lo, mv_hi, start=False, stop=stop)

            def product_quarter(dst, a_hi, a_lo, m_hi, m_lo, q, last_stops=True):
                for t in range(q * QT, (q + 1) * QT):
                    last = three(dst, a_hi[:, t, :], a_lo[:, t, :], m_hi[:, t, :], m_lo[:, t, :],
                                 t == 0, last_stops and t == NB - 1)
                return last

            def project(dst, c0, c1):
                for k in range(KT):
                    last = three(dst, xt_hi[:, k, :], xt_lo[:, k, :], w_hi[:, k, c0:c1], w_lo[:, k, c0:c1],
                                 k == 0, k == KT - 1)
                return last

            pe.wait_ge(id1, 1)

            def step(b, s, has):
                for q in range(NQ):
                    if has[0]:
                        pe.wait_ge(lo_done, NQ * b + q + 1)
                        if isinstance(b, int) and b == 0:
                            pe.wait_ge(xlo_done, q + 1)
                        if q == 0 and (not isinstance(b, int) or b > 1):
                            pe.wait_ge(y_done, b - 1)
                        last = product_quarter(acc[s][:, 0:D], blk_hi, blk_lo, x_hi, x_lo, q)
                        if q == NQ - 1:
                            last.then_inc(acc_done, 1)
                    if has[-1]:
                        if q % 2 == 0:
                            pe.wait_ge(inc_done, 2 * (b + 1) + q // 2 + 1)
                        transpose_quarter(NQ * (b + 1) + q, inc, q)
                    if has[2] and q == 1:
                        pe.wait_ge(xtlo_done, b - 1)
                        if isinstance(b, int) and b == 2:
                            pe.wait_ge(wlo_done, 1)
                            pe.wait_ge(blo_done, 1)
                        else:
                            pe.wait_ge(hlo_done, b - 2)
                            pe.wait_ge(wide_done, b - 2)
                        project(ps_h[:, 0:HC], 0, HC).then_inc(h_done, 1)
                    if has[2] and q == 2:
                        if not isinstance(b, int) or b > 2:
                            pe.wait_ge(glo_done, b - 2)
                        project(ps_g[:, 0:GC], HC, WC).then_inc(g_done, 1)
                    if has[2] and q == 3:
                        if not isinstance(b, int) or b > 2:
                            pe.wait_ge(right_done, b - 2)
                        pe.wait_ge(wide_done, b - 1)
                        nc.tensor.transpose(ps_r[:, 0:P], wide[:, :], ident[:, :]).then_inc(r_done, 1)
                    if has[1] and q == 3:
                        pe.wait_ge(x1n_done, b)
                        if not isinstance(b, int) or b > 1:
                            pe.wait_ge(xtlo_done, b - 1)
                        for k in range(KT):
                            last = nc.tensor.transpose(ps_x[:, k * P:(k + 1) * P], x1_now[:, k * P:(k + 1) * P], ident[:, :])
                        last.then_inc(xt_done, 1)

            def pe_steps():
                def has(b):
                    return {k: 0 <= b - k < NB for k in range(-2, 3)}
                for b in range(-1, 4):
                    step(b, b % 2, has(b))
                with pe.Fori(2, NB // 2 - 1) as t:
                    for s in range(2):
                        step(2 * t + s, s, has(4))
                for b in range(NB - 2, NB + 2):
                    step(b, b % 2, has(b))

            pe_steps()

            pe.wait_ge(ones1, 1)

            def step2(b, s, first, last):
                for q in range(NQ):
                    pe.wait_ge(ctlo_done, NQ * b + q + 1)
                    if q == 0:
                        if first:
                            pe.wait_ge(glo_done, NB - 1)
                            pe.wait_ge(y_done, NB)
                        else:
                            pe.wait_ge(nbp_done, b)
                            pe.wait_ge(zl_done, b)
                    if q == NQ - 1 and first:
                        pe.wait_ge(glo_done, NB)
                    product_quarter(acc[1][:, 0:GC], ct_hi, ct_lo, g_hi, g_lo, q, last_stops=False).then_inc(ctq_used, 1)
                    if q == NQ - 1:
                        nc.tensor.matmul(acc[1][:, 0:GC], first_row[:, :], brow_hi[:, :], start=False, stop=False)
                        nc.tensor.matmul(acc[1][:, 0:GC], first_row[:, :], brow_lo[:, :], start=False,
                                         stop=True).then_inc(ag_done, 1)
                    pe.wait_ge(mask_done, NQ * b + q + 1)
                    transpose_quarter(NQ * NB + NQ * b + q, e[:, s, :], q)
                for q in range(NQ):
                    pe.wait_ge(lo_done, NQ * NB + NQ * b + q + 1)
                    if q == 0:
                        if first:
                            pe.wait_ge(hlo_done, NB)
                        else:
                            pe.wait_ge(z_done, b)
                    last_mm = product_quarter(acc[0][:, 0:D], blk_hi, blk_lo, h_hi, h_lo, q)
                last_mm.then_inc(eh_done, 1)

            steps2(pe, step2)


_OUT = (2048, 256)


def kernel(x, adj, L1_gnn_W_sa, L1_gnn_a_sa, L1_gnn_W_gcnb, L1_gnn_b_gcnb, L1_gnn_Wa, L1_gnn_ba, L1_gnn_Wb, L1_gnn_bb):
    import numpy as np
    import concourse.bacc as bacc
    from concourse import mybir as mb
    from concourse.bass_utils import run_bass_kernel_spmd

    x, adj = np.asarray(x), np.asarray(adj)
    w_sa, w_g = np.asarray(L1_gnn_W_sa), np.asarray(L1_gnn_W_gcnb)
    wa, wb = np.asarray(L1_gnn_Wa), np.asarray(L1_gnn_Wb)
    n, d = x.shape
    gap = np.zeros((d, 1), np.float32)
    adj_t = adj.reshape(n // 128, 128, n // 128, 128).transpose(0, 3, 2, 1).reshape(n // 128, 128, n)
    arrays = {
        "x": x,
        "adj": adj,
        "adj_t": adj_t,
        "w_cat": np.concatenate([w_sa, gap, wa[:, d:].T, wb[:, d:].T, gap, w_g, wa[:, :d].T, wb[:, :d].T], axis=1),
        "a_sa": np.asarray(L1_gnn_a_sa),
        "bias_row": np.concatenate([np.asarray(L1_gnn_b_gcnb), np.asarray(L1_gnn_ba), np.asarray(L1_gnn_bb)])[None],
    }
    arrays = {k: np.ascontiguousarray(v) for k, v in arrays.items()}
    nc = bacc.Bacc("TRN2", target_bir_lowering=False, num_devices=1)
    args = [nc.dram_tensor(k, v.shape, mb.dt.from_np(v.dtype), kind="ExternalInput").ap() for k, v in arrays.items()]
    args.append(nc.dram_tensor("out", _OUT, mb.dt.float32, kind="ExternalOutput").ap())
    two_layer_gnn(nc, *args)
    r = run_bass_kernel_spmd(nc, [arrays], core_ids=[0])
    return r.results[0]["out"]
```

```python
import concourse.bass as bass
from concourse import mybir
from contextlib import ExitStack

P = 128


def two_layer_gnn(nc, x, adj, adj_t, w_cat, a_sa, bias_row, out):
    F32, F32R, BF16, I8 = mybir.dt.float32, mybir.dt.float32r, mybir.dt.bfloat16, mybir.dt.int8
    ALU, ACT = mybir.AluOpType, mybir.ActivationFunctionType

    N, D = x.shape
    NB = N // P
    NQ = 4
    QT = NB // NQ
    QC = QT * P
    HALF = N // 2
    KT = D // P
    HC = D + 4
    EC = D + 2
    GC = D + 2
    WC = HC + GC
    PARTS = 3
    SK = 2 * PARTS
    LN_EPS, COUNT_EPS, SUM_EPS, SLOPE = 1e-5, 1e-24, 1e-5, 0.01

    ctx = ExitStack()
    with ctx:
        def sb(name, shape, dt, stack=None):
            return (stack or ctx).enter_context(nc.sbuf_tensor(name, shape, dt))

        def bank(name):
            return ctx.enter_context(nc.psum_tensor(name, [P, 512], F32))

        def sem(name):
            return ctx.enter_context(nc.semaphore(name))

        h_hi, h_lo = sb("h_hi", [P, NB, EC], F32R), sb("h_lo", [P, NB, EC], F32R)
        g_hi, g_lo = sb("g_hi", [P, NB, GC], F32R), sb("g_lo", [P, NB, GC], F32R)
        x1 = sb("x1", [P, NB, D], F32)
        blk_hi, blk_lo = sb("blk_hi", [P, NB, P], F32R), sb("blk_lo", [P, NB, P], F32R)
        cols = sb("cols", [P, 2, N], F32)
        w_f = sb("w_f", [P, KT, WC], F32)
        w_hi, w_lo = sb("w_hi", [P, KT, WC], F32R), sb("w_lo", [P, KT, WC], F32R)
        a_bc = sb("a_bc", [P, 2 * D], F32)
        xt_hi, xt_lo = sb("xt_hi", [P, KT, P], F32R), sb("xt_lo", [P, KT, P], F32R)
        brow = sb("brow", [P, GC], F32)
        brow_hi, brow_lo = sb("brow_hi", [P, GC], F32R), sb("brow_lo", [P, GC], F32R)
        first_row = sb("first_row", [P, P], F32R)
        ident, ident_bf = sb("ident", [P, P], F32), sb("ident_bf", [P, P], BF16)
        nodecols = sb("nodecols", [P, NB, 4], F32)
        pack = sb("pack", [P, 2 * SK], BF16)
        rest1, rest2 = sb("rest1", [P, 2], F32), sb("rest2", [P, 2], F32)
        score_rows = sb("score_rows", [P, NB, 2, P], BF16)
        minus_half = sb("minus_half", [P, 1], F32)
        plus_half = sb("plus_half", [P, D], F32)
        cnt, cnt2 = sb("cnt", [P, 1], F32), sb("cnt2", [P, 2], F32)
        cnt_g = sb("cnt_g", [P, 1], F32)
        scale = sb("scale", [P, 1], F32)
        deg2 = sb("deg2", [P, 2], F32)
        deg = sb("deg", [P, 1], F32)
        rdeg = sb("rdeg", [P, 2], F32)
        stats, mv = sb("stats", [P, 6], F32), sb("mv", [P, 2], F32)
        var_g, rstd = sb("var_g", [P, 1], F32), sb("rstd", [P, 1], F32)
        y = sb("y", [P, D], F32)
        x1_now = sb("x1_now", [P, D], F32)
        one = ExitStack()
        rows = sb("rows", [P, 2, N], F32, one)
        x_hi, x_lo = sb("x_hi", [P, NB, D], F32R, one), sb("x_lo", [P, NB, D], F32R, one)
        inc = sb("inc", [P, N], F32, one)
        sgn, pos = sb("sgn", [P, N], I8, one), sb("pos", [P, N], I8, one)
        one.close()
        e = sb("e", [P, N], F32)
        e_steep = sb("e_steep", [P, 2, QC], F32)
        sb("unused", [P, N - 2 * QC], F32)
        ct_hi, ct_lo = sb("ct_hi", [P, NB, P], F32R), sb("ct_lo", [P, NB, P], F32R)
        out_sb = sb("out_sb", [P, 2, D], F32)
        nb_part = sb("nb_part", [P, D], F32)
        z, th = sb("z", [P, D], F32), sb("th", [P, D], F32)
        rrow, recip = sb("rrow", [P, 1], F32), sb("recip", [P, 1], F32)
        zl, tl, attn = sb("zl", [P, 2], F32), sb("tl", [P, 2], F32), sb("attn", [P, 2], F32)
        coef = sb("coef", [P, 1], F32)

        turned = [bank("turned0"), bank("turned1")]
        acc = [bank("acc0"), bank("acc1")]
        ps_x, ps_h, ps_g, ps_r = bank("ps_x"), bank("ps_h"), bank("ps_g"), bank("ps_r")

        rows_in = sem("rows_in")
        cols_in = sem("cols_in")
        half_in, half_counted = sem("half_in"), sem("half_counted")
        x_in = [sem(f"x_in{q}") for q in range(NQ)]
        w_in, a_in, b_in = sem("w_in"), sem("a_in"), sem("b_in")
        id0, id1, id_bf = sem("id0"), sem("id1"), sem("id_bf")
        ones0, ones1, h_pad = sem("ones0"), sem("ones1"), sem("h_pad")
        half_set, brow0 = sem("half_set"), sem("brow0")
        xhi_done, xlo_done = sem("xhi_done"), sem("xlo_done")
        sgn_done, cnt_done = sem("sgn_done"), sem("cnt_done")
        cntg_done, scale_done = sem("cntg_done"), sem("scale_done")
        inc_done = sem("inc_done")
        deg_done, rdeg_done = sem("deg_done"), sem("rdeg_done")
        turn_done = sem("turn_done")
        hi_done, lo_done = sem("hi_done"), sem("lo_done")
        acc_done, y_done = sem("acc_done"), sem("y_done")
        xq_used = sem("xq_used")
        st_done, mv_done = sem("st_done"), sem("mv_done")
        varg_done, rstd_done = sem("varg_done"), sem("rstd_done")
        x1n_done, x1_kept = sem("x1n_done"), sem("x1_kept")
        xt_done, xthi_done, xtlo_done = sem("xt_done"), sem("xthi_done"), sem("xtlo_done")
        h_done, g_done, r_done = sem("h_done"), sem("g_done"), sem("r_done")
        hhi_done, hlo_done = sem("hhi_done"), sem("hlo_done")
        ghi_done, glo_done = sem("ghi_done"), sem("glo_done")
        nodecols_done, pack_done = sem("nodecols_done"), sem("pack_done")
        rows_done = sem("rows_done")
        v_done, whi_done, wlo_done = sem("v_done"), sem("whi_done"), sem("wlo_done")
        bhi_done, blo_done = sem("bhi_done"), sem("blo_done")
        score_done, mask_done = sem("score_done"), sem("mask_done")
        flat_done, steep_done, lesser_done = sem("flat_done"), sem("steep_done"), sem("lesser_done")
        ehi_done, elo_done, eq_used = sem("ehi_done"), sem("elo_done"), sem("eq_used")
        cthi_done, ctlo_done, ctq_used = sem("cthi_done"), sem("ctlo_done"), sem("ctq_used")
        ag_done = sem("ag_done")
        zl_done, tl_done, attn_done = sem("zl_done"), sem("tl_done"), sem("attn_done")
        rrow_done, recip_done, coef_done = sem("rrow_done"), sem("recip_done"), sem("coef_done")
        nbp_done, z_done, th_done = sem("nbp_done"), sem("z_done"), sem("th_done")
        y2_done, out_done, out_stored = sem("y2_done"), sem("out_done"), sem("out_stored")

        sp_waits, act_waits, pool_waits, dve_waits, pe_waits = (
            sem("sp_waits"), sem("act_waits"), sem("pool_waits"), sem("dve_waits"), sem("pe_waits"))

        block = ctx.enter_context(nc.Block())

        def once(eng, s, value):
            if not isinstance(value, int) or value > 0:
                eng.wait_ge(s, value)

        def steps(eng, step, first, last):
            lo, hi = 4, NB - 2

            def has(b):
                return {k: 0 <= b - k < NB for k in range(-2, 4)}
            for b in range(first, lo):
                step(b, b % 2, has(b))
            with eng.Fori(lo // 2, hi // 2) as t:
                for s in range(2):
                    step(2 * t + s, s, has(lo))
            for b in range(hi, last + 1):
                step(b, b % 2, has(b))

        def steps2(eng, step):
            step(0, 0, True, False)
            step(1, 1, False, False)
            with eng.Fori(1, NB // 2 - 1) as t:
                for s in range(2):
                    step(2 * t + s, s, False, False)
            step(NB - 2, 0, False, False)
            step(NB - 1, 1, False, True)

        def quarter(t, q):
            return t[:, q * QC:(q + 1) * QC]

        def tiles(t, q):
            return t[:, q * QT:(q + 1) * QT, :].rearrange("p t c -> p (t c)")

        @block.sync
        def _(sp):
            adj_b = adj.rearrange("(b p) n -> b p n", p=P)
            x_v = x.rearrange("(t p) d -> p t d", p=P)
            out_b = out.rearrange("(b p) d -> b p d", p=P)
            def load_x(q):
                sp.dma_start(x1[:, q * QT:(q + 1) * QT, :], x_v[:, q * QT:(q + 1) * QT, :]).then_inc(x_in[q], 16)

            sp.dma_start(rows[:, 0, 0:HALF], adj_b[0][:, 0:HALF]).then_inc(half_in, 16)
            sp.dma_start(rows[:, 0, HALF:N], adj_b[0][:, HALF:N]).then_inc(rows_in, 16)
            load_x(0)
            sp.wait_ge(rows_in, 16)
            sp.dma_start(rows[:, 1, :], adj_b[1]).then_inc(rows_in, 16)
            for q in range(1, NQ):
                load_x(q)
            sp.dma_start(w_f[:, :, :], w_cat.rearrange("(k p) c -> p k c", p=P)).then_inc(w_in, 16)
            sp.dma_start(a_bc[:, :], a_sa.partition_broadcast(P)).then_inc(a_in, 16)
            sp.wait_ge(brow0, 1)
            sp.dma_start(brow[0:1, :], bias_row).then_inc(b_in, 16)
            with sp.Fori(1, NB // 2) as t:
                for s in range(2):
                    b = 2 * t + s
                    sp.wait_ge(rows_in, 16 * b)
                    sp.sem_inc(sp_waits, 1)
                    sp.wait_ge(inc_done, 2 * (b - 2) + 2)
                    sp.sem_inc(sp_waits, 1)
                    sp.dma_start(rows[:, s, :], adj_b[b]).then_inc(rows_in, 16)
            sp.dma_start(cols[:, 0, :], adj_t[0]).then_inc(cols_in, 16)
            sp.wait_ge(cols_in, 16)
            sp.dma_start(cols[:, 1, :], adj_t[1]).then_inc(cols_in, 16)

            def load(b, s):
                sp.wait_ge(cols_in, 16 * b)
                sp.sem_inc(sp_waits, 1)
                sp.wait_ge(ctlo_done, NQ * (b - 2) + NQ)
                sp.sem_inc(sp_waits, 1)
                sp.wait_ge(mask_done, NQ * (b - 2) + NQ)
                sp.sem_inc(sp_waits, 1)
                sp.dma_start(cols[:, s, :], adj_t[b]).then_inc(cols_in, 16)

            def store(b, s, first=False):
                if not first:
                    sp.wait_ge(out_stored, 16 * b)
                    sp.sem_inc(sp_waits, 1)
                sp.wait_ge(out_done, b + 1)
                sp.sem_inc(sp_waits, 1)
                sp.dma_start(out_b[b], out_sb[:, s, :]).then_inc(out_stored, 16)

            LAG = 4
            for b in range(2, LAG + 2):
                load(b, b % 2)
                if b >= LAG:
                    store(b - LAG, b % 2, first=b == LAG)
            with sp.Fori(LAG // 2 + 1, NB // 2) as t:
                for s in range(2):
                    load(2 * t + s, s)
                    store(2 * t + s - LAG, s)
            for b in range(NB - LAG, NB):
                store(b, b % 2)
            sp.wait_ge(out_stored, 16 * NB)

        @block.gpsimd
        def _(pool):
            pool.memset(ident[:, :], 0.0).then_inc(id0, 1)
            pool.memset(minus_half[:, :], -0.5).then_inc(half_set, 1)
            pool.memset(plus_half[:, :], 0.5).then_inc(half_set, 1)
            pool.memset(first_row[:, :].bitcast(F32), 0.0).then_inc(ones0, 1)
            pool.memset(brow[:, :], 0.0).then_inc(brow0, 1)
            pool.wait_ge(id0, 1)
            pool.affine_select(out=ident[:, :], in_=ident[:, :], compare_op=ALU.not_equal, fill=1.0, base=0,
                               pattern=[[-1, P]], channel_multiplier=1).then_inc(id1, 1)
            pool.wait_ge(ones0, 1)
            pool.memset(first_row[0:1, :].bitcast(F32), 1.0).then_inc(ones1, 1)
            pool.memset(pack[:, :], 1.0).then_inc(h_pad, 1)
            pool.memset(h_hi[:, :, D:D + 1].bitcast(F32), 1.0).then_inc(h_pad, 1)
            pool.memset(h_hi[:, :, D + 1:D + 2].bitcast(F32), 0.0).then_inc(h_pad, 1)
            pool.memset(h_lo[:, :, D:D + 2].bitcast(F32), 0.0).then_inc(h_pad, 1)
            pool.wait_ge(id1, 1)
            pool.tensor_copy(ident_bf[:, :], ident[:, :]).then_inc(id_bf, 1)
            pool.wait_ge(half_set, 2)
            pool.wait_ge(h_pad, 4)

            def rsqrt_of_var(n, phase1):
                once(pool, rstd_done, n)
                pool.wait_ge(mv_done, n + 1)
                pool.sem_inc(pool_waits, 1)
                pool.tensor_scalar(var_g[:, :], mv[:, 1:2], LN_EPS, 1.0, ALU.add, ALU.mult).then_inc(varg_done, 1)
                pool.wait_ge(varg_done, n + 1)
                once(pool, x1n_done, n if phase1 else NB)
                if not phase1:
                    once(pool, out_done, n - NB)
                pool.tensor_tensor(rstd[:, :], var_g[:, :], minus_half[:, :], ALU.pow).then_inc(rstd_done, 1)

            def parts_of_scores(b):
                def part(k):
                    return pack[:, PARTS + k:2 * PARTS + k + 1:PARTS]

                once(pool, r_done, b)
                pool.wait_ge(nodecols_done, b + 1)
                pool.sem_inc(pool_waits, 1)
                pool.tensor_copy(part(0), nodecols[:, b, 0:2]).then_inc(pack_done, 1)
                pool.wait_ge(pack_done, 5 * b + 1)
                pool.sem_inc(pool_waits, 1)
                pool.tensor_tensor(rest1[:, :], nodecols[:, b, 0:2], part(0), ALU.subtract).then_inc(pack_done, 1)
                pool.wait_ge(pack_done, 5 * b + 2)
                pool.sem_inc(pool_waits, 1)
                pool.tensor_copy(part(1), rest1[:, :]).then_inc(pack_done, 1)
                pool.wait_ge(pack_done, 5 * b + 3)
                pool.sem_inc(pool_waits, 1)
                pool.tensor_tensor(rest2[:, :], rest1[:, :], part(1), ALU.subtract).then_inc(pack_done, 1)
                pool.wait_ge(pack_done, 5 * b + 4)
                pool.sem_inc(pool_waits, 1)
                pool.tensor_copy(part(2), rest2[:, :]).then_inc(pack_done, 1)

            def keep_x1(b):
                pool.wait_ge(x1n_done, b + 1)
                pool.sem_inc(pool_waits, 1)
                pool.tensor_tensor(x1[:, b, :], x1_now[:, :], plus_half[:, :], ALU.add).then_inc(x1_kept, 1)

            def x_to_lo(q):
                pool.wait_ge(xhi_done, q + 1)
                pool.wait_ge(xlo_done, q)
                t = slice(q * QT, (q + 1) * QT)
                pool.tensor_tensor(x_lo[:, t, :], x1[:, t, :], x_hi[:, t, :].bitcast(F32), ALU.subtract).then_inc(xlo_done, 1)

            def step(b, s, has):
                if has[1]:
                    rsqrt_of_var(b - 1, True)
                if has[-2]:
                    once(pool, scale_done, b + 2)
                    pool.wait_ge(cnt_done, b + 3)
                    pool.sem_inc(pool_waits, 1)
                    pool.tensor_scalar(cnt_g[:, :], cnt[:, :], float(2 * N), COUNT_EPS, ALU.min, ALU.max).then_inc(cntg_done, 1)
                    pool.wait_ge(cntg_done, b + 3)
                    once(pool, inc_done, 2 * (b + 1) + 2 if not isinstance(b, int) or b > -2 else 0)
                    pool.tensor_tensor(scale[:, :], cnt_g[:, :], minus_half[:, :], ALU.pow).then_inc(scale_done, 1)
                if isinstance(b, int) and b == -1:
                    x_to_lo(2)
                    x_to_lo(3)
                if has[1]:
                    keep_x1(b - 1)
                if isinstance(b, int) and b == 1:
                    pool.wait_ge(whi_done, 1)
                    pool.tensor_tensor(w_lo[:, :, :], w_f[:, :, :], w_hi[:, :, :].bitcast(F32), ALU.subtract).then_inc(wlo_done, 1)
                    pool.wait_ge(bhi_done, 1)
                    pool.tensor_tensor(brow_lo[:, :], brow[:, :], brow_hi[:, :].bitcast(F32), ALU.subtract).then_inc(blo_done, 1)
                if has[2]:
                    parts_of_scores(b - 2)

            steps(pool, step, -2, NB - 1)

            def cols_lo(b, s, q):
                pool.wait_ge(cthi_done, NQ * b + q + 1)
                pool.sem_inc(pool_waits, 1)
                if isinstance(b, int) and b == 0:
                    pool.wait_ge(xq_used, NQ // 2 + q // 2 + 1)
                    pool.wait_ge(ctlo_done, q)
                pool.tensor_tensor(tiles(ct_lo, q), quarter(cols[:, s, :], q), tiles(ct_hi, q).bitcast(F32),
                                   ALU.subtract).then_inc(ctlo_done, 1)

            L = NB - 1
            rsqrt_of_var(L, True)
            cols_lo(0, 0, 1)
            keep_x1(L)
            parts_of_scores(L - 1)
            cols_lo(0, 0, 2)
            parts_of_scores(L)

            def step2(b, s, first, last):
                if not first:
                    rsqrt_of_var(NB + b - 1, False)
                if not last:
                    for q in range(NQ):
                        cols_lo(b + 1, 1 - s, q)

            steps2(pool, step2)
            rsqrt_of_var(2 * NB - 1, False)

        @block.scalar
        def _(act):
            def split_hi(n, q):
                act.wait_ge(turn_done, n + 1)
                nc.scalar.copy(tiles(blk_hi, q), turned[q % 2][:, :]).then_inc(hi_done, 1)

            def signs(b, s):
                act.wait_ge(rows_in, 16 * (b + 1))
                once(act, cnt_done, b)
                nc.scalar.activation(sgn[:, :], rows[:, s, :], ACT.Sign).then_inc(sgn_done, 1)

            def positives(b):
                act.wait_ge(sgn_done, b)
                act.wait_ge(inc_done, 2 * b)
                act.wait_ge(cntg_done, b)
                nc.scalar.activation(pos[:, :], sgn[:, :], ACT.Relu, accum_out=cnt[:, :]).then_inc(cnt_done, 1)

            def x_to_hi(q):
                act.wait_ge(x_in[q], 16)
                nc.scalar.copy(x_hi[:, q * QT:(q + 1) * QT, :], x1[:, q * QT:(q + 1) * QT, :]).then_inc(xhi_done, 1)

            def turned_x1_hi(b):
                act.wait_ge(xt_done, b + 1)
                nc.scalar.copy(xt_hi[:, :, :].rearrange("p k c -> p (k c)"), ps_x[:, 0:D]).then_inc(xthi_done, 1)

            def h_to_hi(b):
                act.wait_ge(h_done, b + 1)
                act.sem_inc(act_waits, 1)
                nc.scalar.copy(h_hi[:, b, 0:D], ps_h[:, 0:D]).then_inc(hhi_done, 1)

            def g_to_hi(b):
                act.wait_ge(g_done, b + 1)
                act.sem_inc(act_waits, 1)
                nc.scalar.copy(g_hi[:, b, :], ps_g[:, 0:GC]).then_inc(ghi_done, 1)

            def rows_of_scores(b):
                act.wait_ge(r_done, b + 1)
                act.sem_inc(act_waits, 1)
                nc.scalar.copy(score_rows[0:SK, b, :, :].rearrange("p i c -> p (i c)"), ps_r[0:SK, 0:2 * P]).then_inc(rows_done, 1)

            def step(b, s, has):
                if isinstance(b, int) and b == -2:
                    x_to_hi(0)
                    return
                if isinstance(b, int) and b == -1:
                    signs(1, 1)
                for q in range(NQ):
                    if has[2] and q == 0:
                        turned_x1_hi(b - 2)
                    if has[-1]:
                        split_hi(NQ * (b + 1) + q, q)
                    if has[-2] and q == 0 and not (isinstance(b, int) and b == -1):
                        signs(b + 2, s)
                    if has[-2] and q == 1:
                        positives(b + 2)
                    if isinstance(b, int) and b == -1 and q > 0:
                        x_to_hi(q)
                    if isinstance(b, int) and b == 0 and q == 3:
                        act.wait_ge(v_done, 2 * KT)
                        nc.scalar.copy(w_hi[:, :, :], w_f[:, :, :]).then_inc(whi_done, 1)
                        act.wait_ge(b_in, 16)
                        nc.scalar.copy(brow_hi[:, :], brow[:, :]).then_inc(bhi_done, 1)
                    if has[2] and q == 2:
                        h_to_hi(b - 2)
                    if has[2] and q == 3:
                        g_to_hi(b - 2)
                    if has[3] and q == 2:
                        rows_of_scores(b - 3)

            steps(act, step, -2, NB - 2)

            def exps(b, q):
                act.wait_ge(score_done, NQ * b + q + 1)
                if isinstance(b, int) and b == 0:
                    act.wait_ge(inc_done, 2 * NB)
                else:
                    act.wait_ge(elo_done, NQ * (b - 1) + q + 1)
                nc.scalar.activation(quarter(e, q), turned[q % 2][:, :], ACT.Exp, scale=-SLOPE).then_inc(flat_done, 1)
                if not isinstance(b, int) or b > 0 or q > 1:
                    act.wait_ge(lesser_done, NQ * b + q - 1)
                nc.scalar.activation(e_steep[:, q % 2, :], turned[q % 2][:, :], ACT.Exp, scale=-1.0).then_inc(steep_done, 1)

            def e_hi(b, q):
                act.wait_ge(mask_done, NQ * b + q + 1)
                if isinstance(b, int) and b == 0:
                    act.wait_ge(xq_used, NQ)
                else:
                    act.wait_ge(eq_used, NQ * (b - 1) + q + 1)
                nc.scalar.copy(tiles(blk_hi, q), quarter(e, q)).then_inc(ehi_done, 1)

            def cols_hi(b, s, q):
                if q == 0:
                    act.wait_ge(cols_in, 16 * (b + 1))
                if isinstance(b, int) and b == 0:
                    act.wait_ge(xq_used, q // 2 + 1)
                else:
                    act.wait_ge(ctq_used, NQ * (b - 1) + q + 1)
                nc.scalar.copy(tiles(ct_hi, q), quarter(cols[:, s, :], q)).then_inc(cthi_done, 1)

            def gates(b):
                once(act, attn_done, b)
                act.wait_ge(zl_done, b + 1)
                nc.scalar.activation(tl[:, :], zl[:, :], ACT.Tanh, scale=0.5).then_inc(tl_done, 1)

            def neighbours(b):
                once(act, z_done, b)
                act.wait_ge(attn_done, b + 1)
                nc.scalar.activation(nb_part[:, :], acc[1][:, 0:D], ACT.Copy, scale=attn[:, 1:2]).then_inc(nbp_done, 1)

            def final(b):
                once(act, y2_done, b)
                act.wait_ge(z_done, b + 1)
                nc.scalar.activation(th[:, :], z[:, :], ACT.Tanh, scale=0.5).then_inc(th_done, 1)

            L = NB - 1
            turned_x1_hi(L - 2)
            rows_of_scores(L - 3)
            exps(0, 0)
            h_to_hi(L - 2)
            g_to_hi(L - 2)
            cols_hi(0, 0, 0)
            turned_x1_hi(L - 1)
            cols_hi(0, 0, 1)
            rows_of_scores(L - 2)
            exps(0, 1)
            h_to_hi(L - 1)
            exps(0, 2)
            g_to_hi(L - 1)
            cols_hi(0, 0, 2)
            turned_x1_hi(L)
            e_hi(0, 0)
            h_to_hi(L)
            cols_hi(0, 0, 3)
            g_to_hi(L)
            rows_of_scores(L - 1)
            e_hi(0, 1)
            rows_of_scores(L)
            e_hi(0, 2)
            exps(0, 3)
            cols_hi(1, 1, 0)
            e_hi(0, 3)

            def step2(b, s, first, last):
                s1 = 1 - s
                if not first:
                    e_hi(b, 0)
                    e_hi(b, 1)
                    e_hi(b, 2)
                    final(b - 1)
                    if not last:
                        cols_hi(b + 1, s1, 0)
                    e_hi(b, 3)
                    if not last:
                        cols_hi(b + 1, s1, 1)
                if last:
                    gates(b)
                    neighbours(b)
                else:
                    exps(b + 1, 0)
                    if first:
                        cols_hi(b + 1, s1, 1)
                    gates(b)
                    cols_hi(b + 1, s1, 2)
                    neighbours(b)
                    exps(b + 1, 1)
                    cols_hi(b + 1, s1, 3)
                    exps(b + 1, 2)
                    exps(b + 1, 3)

            steps2(act, step2)
            final(NB - 1)

        @block.vector
        def _(dve):
            def split_lo(n, q):
                dve.wait_ge(hi_done, n + 1)
                nc.vector.tensor_tensor(tiles(blk_lo, q), turned[q % 2][:, :], tiles(blk_hi, q).bitcast(F32),
                                        ALU.subtract).then_inc(lo_done, 1)

            def build_inc(b, s, half):
                if half == 0:
                    dve.wait_ge(scale_done, b + 1)
                if not isinstance(b, int) or b > 0:
                    dve.wait_ge(turn_done, NQ * (b - 1) + 2 * half + 2)
                    if half == 0:
                        dve.wait_ge(deg_done, b)
                c = slice(half * HALF, (half + 1) * HALF)
                nc.vector.scalar_tensor_tensor(out=inc[:, c], in0=pos[:, c], scalar=scale[:, :], in1=rows[:, s, c],
                                               op0=ALU.mult, op1=ALU.add, accum_out=deg2[:, half:half + 1]).then_inc(inc_done, 1)

            def layer_norm_stats(n):
                once(dve, mv_done, n)
                nc.vector.bn_stats(stats[:, :], y[:, :]).then_inc(st_done, 1)

            def layer_norm_moments(n):
                once(dve, varg_done, n)
                dve.wait_ge(st_done, n + 1)
                dve.sem_inc(dve_waits, 1)
                nc.vector.bn_aggr(mv[:, :], stats[:, :]).then_inc(mv_done, 1)

            def x_to_lo(q):
                dve.wait_ge(xhi_done, q + 1)
                t = slice(q * QT, (q + 1) * QT)
                nc.vector.tensor_tensor(x_lo[:, t, :], x1[:, t, :], x_hi[:, t, :].bitcast(F32),
                                        ALU.subtract).then_inc(xlo_done, 1)

            def residual(b, s):
                once(dve, x1n_done, b)
                dve.wait_ge(rdeg_done, b + 1)
                if isinstance(b, int) and b == NB - 1:
                    dve.wait_ge(xq_used, NQ)
                else:
                    dve.wait_ge(acc_done, b + 1)
                nc.vector.scalar_tensor_tensor(out=y[:, :], in0=acc[s][:, 0:D], scalar=rdeg[:, s:s + 1],
                                               in1=x1[:, b, :], op0=ALU.mult, op1=ALU.add).then_inc(y_done, 1)

            def turned_x1_lo(b):
                dve.wait_ge(xthi_done, b + 1)
                nc.vector.tensor_tensor(xt_lo[:, :, :].rearrange("p k c -> p (k c)"), ps_x[:, 0:D],
                                        xt_hi[:, :, :].rearrange("p k c -> p (k c)").bitcast(F32),
                                        ALU.subtract).then_inc(xtlo_done, 1)

            def normed(b):
                dve.wait_ge(rstd_done, b + 1)
                once(dve, xt_done, b)
                once(dve, x1_kept, b)
                nc.vector.tensor_scalar(x1_now[:, :], y[:, :], mv[:, 0:1], rstd[:, :], ALU.subtract,
                                        ALU.mult).then_inc(x1n_done, 1)

            def h_rest(b):
                dve.wait_ge(hhi_done, b + 1)
                nc.vector.tensor_copy(nodecols[:, b, :], ps_h[:, D:HC]).then_inc(nodecols_done, 1)
                nc.vector.tensor_tensor(h_lo[:, b, 0:D], ps_h[:, 0:D], h_hi[:, b, 0:D].bitcast(F32),
                                        ALU.subtract).then_inc(hlo_done, 1)

            def g_rest(b):
                dve.wait_ge(ghi_done, b + 1)
                nc.vector.tensor_tensor(g_lo[:, b, :], ps_g[:, 0:GC], g_hi[:, b, :].bitcast(F32),
                                        ALU.subtract).then_inc(glo_done, 1)

            def step(b, s, has):
                if isinstance(b, int) and b == -2:
                    for half, arrived in enumerate((half_in, rows_in)):
                        dve.wait_ge(arrived, 16)
                        c = slice(half * HALF, (half + 1) * HALF)
                        nc.vector.tensor_scalar(pos[:, c], rows[:, 0, c], 0.0, None, ALU.is_gt, ALU.add,
                                                accum_out=cnt2[:, half:half + 1]).then_inc(half_counted, 1)
                    dve.wait_ge(half_counted, 2)
                    nc.vector.tensor_tensor(cnt[:, :], cnt2[:, 0:1], cnt2[:, 1:2], ALU.add).then_inc(cnt_done, 1)
                if has[1]:
                    residual(b - 1, 1 - s)
                if has[2]:
                    turned_x1_lo(b - 2)
                if has[1]:
                    dve.wait_ge(y_done, b)
                    layer_norm_stats(b - 1)
                    layer_norm_moments(b - 1)
                if has[-1]:
                    build_inc(b + 1, 1 - s, 1)
                if has[-1]:
                    split_lo(NQ * (b + 1), 0)
                    dve.wait_ge(inc_done, 2 * (b + 1) + 2)
                    once(dve, rdeg_done, b + 1)
                    nc.vector.tensor_tensor(deg[:, :], deg2[:, 0:1], deg2[:, 1:2], ALU.add).then_inc(deg_done, 1)
                if has[-1]:
                    once(dve, y_done, b)
                    dve.wait_ge(deg_done, b + 2)
                    nc.vector.reciprocal(rdeg[:, 1 - s:2 - s], deg[:, :]).then_inc(rdeg_done, 1)
                    split_lo(NQ * (b + 1) + 1, 1)
                if isinstance(b, int) and b == -1:
                    x_to_lo(1)
                if isinstance(b, int) and b == 0:
                    dve.wait_ge(w_in, 16)
                    dve.wait_ge(a_in, 16)
                    for k in range(KT):
                        for i, to in enumerate((w_f[:, k, D:D + 1], w_f[:, k, D + 1:D + 2])):
                            n = 2 * k + i
                            once(dve, v_done, n)
                            nc.vector.scalar_tensor_tensor(out=products, in0=w_f[:, k, 0:D], scalar=1.0,
                                                           in1=a_bc[:, i * D:(i + 1) * D], op0=ALU.mult, op1=ALU.mult,
                                                           accum_out=to).then_inc(v_done, 1)
                if has[1]:
                    normed(b - 1)
                if has[-1]:
                    split_lo(NQ * (b + 1) + 2, 2)
                if has[-2]:
                    build_inc(b + 2, s, 0)
                if has[2]:
                    h_rest(b - 2)
                if has[-1]:
                    split_lo(NQ * (b + 1) + 3, 3)
                if has[2]:
                    g_rest(b - 2)
                if isinstance(b, int) and b == -2:
                    x_to_lo(0)

            products = h_lo[:, 0, 0:D]
            steps(dve, step, -2, NB - 2)

            def lesser(b, q):
                dve.wait_ge(flat_done, NQ * b + q + 1)
                dve.wait_ge(steep_done, NQ * b + q + 1)
                nc.vector.tensor_tensor(quarter(e, q), quarter(e, q), e_steep[:, q % 2, :], ALU.min).then_inc(lesser_done, 1)

            def mask(b, s, q):
                dve.wait_ge(lesser_done, NQ * b + q + 1)
                if q == 0:
                    dve.wait_ge(cols_in, 16 * (b + 1))
                nc.vector.scalar_tensor_tensor(out=quarter(e, q), in0=quarter(cols[:, s, :], q), scalar=0.0,
                                               in1=quarter(e, q), op0=ALU.not_equal, op1=ALU.mult).then_inc(mask_done, 1)

            def e_lo(b, q):
                dve.wait_ge(ehi_done, NQ * b + q + 1)
                nc.vector.tensor_tensor(tiles(blk_lo, q), quarter(e, q), tiles(blk_hi, q).bitcast(F32),
                                        ALU.subtract).then_inc(elo_done, 1)

            def cols_lo(b, s, q):
                dve.wait_ge(cthi_done, NQ * b + q + 1)
                if isinstance(b, int) and b == 0:
                    dve.wait_ge(xq_used, NQ // 2 + q // 2 + 1)
                nc.vector.tensor_tensor(tiles(ct_lo, q), quarter(cols[:, s, :], q), tiles(ct_hi, q).bitcast(F32),
                                        ALU.subtract).then_inc(ctlo_done, 1)

            def logits(b):
                once(dve, tl_done, b)
                dve.wait_ge(ag_done, b + 1)
                nc.vector.tensor_tensor(zl[:, :], acc[1][:, D:D + 2], nodecols[:, b, 2:4], ALU.add).then_inc(zl_done, 1)

            def attention(b):
                once(dve, coef_done, b)
                once(dve, nbp_done, b)
                dve.wait_ge(tl_done, b + 1)
                nc.vector.tensor_scalar(attn[:, :], tl[:, :], 0.5, 0.5, ALU.mult, ALU.add).then_inc(attn_done, 1)

            def rowsum(b):
                once(dve, recip_done, b)
                dve.wait_ge(eq_used, NQ * b + NQ)
                nc.vector.tensor_scalar(rrow[:, :], acc[0][:, D:D + 1], SUM_EPS, None, ALU.add).then_inc(rrow_done, 1)

            def reciprocal(b):
                dve.wait_ge(rrow_done, b + 1)
                once(dve, coef_done, b)
                nc.vector.reciprocal(recip[:, :], rrow[:, :]).then_inc(recip_done, 1)

            def coefficient(b):
                dve.wait_ge(recip_done, b + 1)
                once(dve, z_done, b)
                nc.vector.tensor_tensor(coef[:, :], recip[:, :], attn[:, 0:1], ALU.mult).then_inc(coef_done, 1)

            def combine(b):
                once(dve, th_done, b)
                dve.wait_ge(nbp_done, b + 1)
                dve.wait_ge(coef_done, b + 1)
                nc.vector.scalar_tensor_tensor(out=z[:, :], in0=acc[0][:, 0:D], scalar=coef[:, :], in1=nb_part[:, :],
                                               op0=ALU.mult, op1=ALU.add).then_inc(z_done, 1)

            def sigmoid_sum(b):
                dve.wait_ge(th_done, b + 1)
                once(dve, out_done, b)
                nc.vector.scalar_tensor_tensor(out=y[:, :], in0=th[:, :], scalar=0.5, in1=x1[:, b, :],
                                               op0=ALU.mult, op1=ALU.add).then_inc(y2_done, 1)

            def finish(b, s):
                dve.wait_ge(rstd_done, NB + b + 1)
                if not isinstance(b, int) or b > 1:
                    dve.wait_ge(out_stored, 16 * (b - 1))
                nc.vector.tensor_scalar(out_sb[:, s, :], y[:, :], mv[:, 0:1], rstd[:, :], ALU.subtract,
                                        ALU.mult).then_inc(out_done, 1)

            L = NB - 1
            residual(L - 1, (L - 1) % 2)
            turned_x1_lo(L - 2)
            dve.wait_ge(y_done, L)
            layer_norm_stats(L - 1)
            layer_norm_moments(L - 1)
            lesser(0, 0)
            normed(L - 1)
            h_rest(L - 2)
            g_rest(L - 2)
            mask(0, 0, 0)
            turned_x1_lo(L - 1)
            cols_lo(0, 0, 0)
            residual(L, L % 2)
            dve.wait_ge(y_done, L + 1)
            layer_norm_stats(L)
            layer_norm_moments(L)
            lesser(0, 1)
            lesser(0, 2)
            normed(L)
            h_rest(L - 1)
            g_rest(L - 1)
            mask(0, 0, 1)
            turned_x1_lo(L)
            mask(0, 0, 2)
            e_lo(0, 0)
            h_rest(L)
            dve.wait_ge(ctlo_done, NQ - 1)
            cols_lo(0, 0, NQ - 1)
            g_rest(L)
            e_lo(0, 1)
            e_lo(0, 2)
            lesser(0, 3)
            mask(0, 0, 3)
            e_lo(0, 3)

            def step2(b, s, first, last):
                s1 = 1 - s
                if not first:
                    rowsum(b - 1)
                    mask(b, s, 2)
                    reciprocal(b - 1)
                    lesser(b, 3)
                    coefficient(b - 1)
                    e_lo(b, 0)
                    combine(b - 1)
                    mask(b, s, 3)
                    e_lo(b, 1)
                    sigmoid_sum(b - 1)
                    e_lo(b, 2)
                    dve.wait_ge(y2_done, b)
                    layer_norm_stats(NB + b - 1)
                    e_lo(b, 3)
                    layer_norm_moments(NB + b - 1)
                    finish(b - 1, s1)
                logits(b)
                if last:
                    attention(b)
                else:
                    lesser(b + 1, 0)
                    attention(b)
                    mask(b + 1, s1, 0)
                    lesser(b + 1, 1)
                    mask(b + 1, s1, 1)
                    lesser(b + 1, 2)

            steps2(dve, step2)
            rowsum(L)
            reciprocal(L)
            coefficient(L)
            combine(L)
            sigmoid_sum(L)
            dve.wait_ge(y2_done, NB)
            layer_norm_stats(NB + L)
            layer_norm_moments(NB + L)
            finish(L, L % 2)

        @block.tensor
        def _(pe):
            def transpose_quarter(n, src, q):
                if not isinstance(n, int) or n >= 2:
                    pe.wait_ge(lo_done, n - 1)
                for t in range(QT):
                    last = nc.tensor.transpose(turned[q % 2][:, t * P:(t + 1) * P],
                                               src[:, (q * QT + t) * P:(q * QT + t + 1) * P], ident[:, :])
                last.then_inc(turn_done, 1)

            def three(dst, hi, lo, mv_hi, mv_lo, start, stop):
                nc.tensor.matmul(dst, hi, mv_hi, start=start, stop=False)
                nc.tensor.matmul(dst, hi, mv_lo, start=False, stop=False)
                return nc.tensor.matmul(dst, lo, mv_hi, start=False, stop=stop)

            def product_quarter(dst, a_hi, a_lo, m_hi, m_lo, q, last_stops=True):
                for t in range(q * QT, (q + 1) * QT):
                    last = three(dst, a_hi[:, t, :], a_lo[:, t, :], m_hi[:, t, :], m_lo[:, t, :],
                                 t == 0, last_stops and t == NB - 1)
                return last

            def project(dst, c0, c1):
                for k in range(KT):
                    last = three(dst, xt_hi[:, k, :], xt_lo[:, k, :], w_hi[:, k, c0:c1], w_lo[:, k, c0:c1],
                                 k == 0, k == KT - 1)
                return last

            pe.wait_ge(id1, 1)

            def projections_h(b):
                pe.wait_ge(xtlo_done, b + 1)
                if isinstance(b, int) and b == 0:
                    pe.wait_ge(wlo_done, 1)
                    pe.wait_ge(blo_done, 1)
                else:
                    pe.wait_ge(hlo_done, b)
                project(ps_h[:, 0:HC], 0, HC).then_inc(h_done, 1)

            def projections_g(b):
                once(pe, glo_done, b)
                project(ps_g[:, 0:GC], HC, WC).then_inc(g_done, 1)

            def turn_parts(b):
                once(pe, rows_done, b)
                if isinstance(b, int) and b == 0:
                    pe.wait_ge(id_bf, 1)
                pe.wait_ge(pack_done, 5 * b + 5)
                nc.tensor.matmul(ps_r[0:SK, 0:P], pack[:, 0:SK], ident_bf[:, :], start=True, stop=True)
                nc.tensor.matmul(ps_r[0:SK, P:2 * P], pack[:, SK:2 * SK], ident_bf[:, :], start=True,
                                 stop=True).then_inc(r_done, 1)

            def turn_x1(b):
                pe.wait_ge(x1n_done, b + 1)
                once(pe, xtlo_done, b)
                for k in range(KT):
                    last = nc.tensor.transpose(ps_x[:, k * P:(k + 1) * P], x1_now[:, k * P:(k + 1) * P], ident[:, :])
                last.then_inc(xt_done, 1)

            def inc_product(b, s, q):
                pe.wait_ge(lo_done, NQ * b + q + 1)
                if isinstance(b, int) and b == 0:
                    pe.wait_ge(xlo_done, q + 1)
                if q == 0 and (not isinstance(b, int) or b > 1):
                    pe.wait_ge(y_done, b - 1)
                last = product_quarter(acc[s][:, 0:D], blk_hi, blk_lo, x_hi, x_lo, q)
                if isinstance(b, int) and b == NB - 1:
                    last.then_inc(xq_used, 1)
                elif q == NQ - 1:
                    last.then_inc(acc_done, 1)

            def step(b, s, has):
                for q in range(NQ):
                    if has[0]:
                        inc_product(b, s, q)
                    if has[3] and q == 1:
                        turn_parts(b - 3)
                    if has[-1]:
                        if q % 2 == 0:
                            pe.wait_ge(inc_done, 2 * (b + 1) + q // 2 + 1)
                        transpose_quarter(NQ * (b + 1) + q, inc, q)
                    if has[2] and q == 1:
                        projections_h(b - 2)
                    if has[2] and q == 2:
                        projections_g(b - 2)
                    if has[1] and q == 3:
                        turn_x1(b - 1)

            def has(b):
                return {k: 0 <= b - k < NB for k in range(-2, 4)}
            for b in range(-1, 4):
                step(b, b % 2, has(b))
            with pe.Fori(2, NB // 2 - 1) as t:
                for s in range(2):
                    step(2 * t + s, s, has(4))
            step(NB - 2, 0, has(NB - 2))

            def scores(b, q):
                if isinstance(b, int) and b == 0:
                    pe.wait_ge(rows_done, QT * (q + 1))
                if isinstance(b, int) and b == 0 and q < 2:
                    pe.wait_ge(lo_done, NQ * NB - 1 + q)
                else:
                    pe.wait_ge(steep_done, NQ * b + q - 1)
                pe.sem_inc(pe_waits, 1)
                for t in range(QT):
                    last = nc.tensor.matmul(turned[q % 2][:, t * P:(t + 1) * P], score_rows[0:SK, q * QT + t, 1, :],
                                            score_rows[0:SK, b, 0, :], start=True, stop=True)
                last.then_inc(score_done, 1)

            def ag_product(b, q):
                pe.wait_ge(ctlo_done, NQ * b + q + 1)
                if isinstance(b, int) and b == 0:
                    pe.wait_ge(glo_done, QT * (q + 1))
                    if q == 0:
                        pe.wait_ge(y_done, NB)
                elif q == 0:
                    pe.wait_ge(nbp_done, b)
                    pe.wait_ge(zl_done, b)
                product_quarter(acc[1][:, 0:GC], ct_hi, ct_lo, g_hi, g_lo, q, last_stops=False).then_inc(ctq_used, 1)
                if q == NQ - 1:
                    nc.tensor.matmul(acc[1][:, 0:GC], first_row[:, :], brow_hi[:, :], start=False, stop=False)
                    nc.tensor.matmul(acc[1][:, 0:GC], first_row[:, :], brow_lo[:, :], start=False,
                                     stop=True).then_inc(ag_done, 1)

            def eh_product(b, q):
                pe.wait_ge(elo_done, NQ * b + q + 1)
                if isinstance(b, int) and b == 0:
                    pe.wait_ge(hlo_done, QT * (q + 1))
                    if q == 0:
                        pe.wait_ge(h_pad, 4)
                elif q == 0:
                    pe.wait_ge(z_done, b)
                last = product_quarter(acc[0][:, 0:EC], blk_hi, blk_lo, h_hi, h_lo, q)
                last.then_inc(eq_used, 1)

            L = NB - 1
            inc_product(L, L % 2, 0)
            turn_parts(L - 3)
            scores(0, 0)
            inc_product(L, L % 2, 1)
            projections_h(L - 2)
            scores(0, 1)
            inc_product(L, L % 2, 2)
            projections_g(L - 2)
            turn_x1(L - 1)
            inc_product(L, L % 2, 3)
            turn_parts(L - 2)
            scores(0, 2)
            projections_h(L - 1)
            projections_g(L - 1)
            pe.wait_ge(ones1, 1)
            ag_product(0, 0)
            turn_x1(L)
            ag_product(0, 1)
            projections_h(L)
            projections_g(L)
            turn_parts(L - 1)
            ag_product(0, 2)
            turn_parts(L)
            ag_product(0, 3)

            def step2(b, s, first, last):
                if not first:
                    for q in range(NQ):
                        ag_product(b, q)
                        if isinstance(b, int) and b == 1 and q < 2:
                            scores(b, q + 2)
                if first:
                    then = [(0, 0, 3), (1, 1, 0), (3, 1, 1)]
                elif last:
                    then = []
                else:
                    then = [(0, b + 1, 0), (0, b + 1, 1), (3, b + 1, 2), (4, b + 1, 3)]
                for q in range(NQ + 1):
                    for at, block_of, quarter_of in then:
                        if at == q:
                            scores(block_of, quarter_of)
                    if q < NQ:
                        eh_product(b, q)

            steps2(pe, step2)


_OUT = (2048, 256)


def kernel(x, adj, L1_gnn_W_sa, L1_gnn_a_sa, L1_gnn_W_gcnb, L1_gnn_b_gcnb, L1_gnn_Wa, L1_gnn_ba, L1_gnn_Wb, L1_gnn_bb):
    import numpy as np
    import concourse.bacc as bacc
    from concourse import mybir as mb
    from concourse.bass_utils import run_bass_kernel_spmd

    x, adj = np.asarray(x), np.asarray(adj)
    w_sa, w_g = np.asarray(L1_gnn_W_sa), np.asarray(L1_gnn_W_gcnb)
    wa, wb = np.asarray(L1_gnn_Wa), np.asarray(L1_gnn_Wb)
    n, d = x.shape
    gap = np.zeros((d, 1), np.float32)
    adj_t = adj.reshape(n // 128, 128, n // 128, 128).transpose(0, 3, 2, 1).reshape(n // 128, 128, n)
    arrays = {
        "x": x,
        "adj": adj,
        "adj_t": adj_t,
        "w_cat": np.concatenate([w_sa, gap, gap, wa[:, d:].T, wb[:, d:].T, w_g, wa[:, :d].T, wb[:, :d].T], axis=1),
        "a_sa": np.asarray(L1_gnn_a_sa),
        "bias_row": np.concatenate([np.asarray(L1_gnn_b_gcnb), np.asarray(L1_gnn_ba), np.asarray(L1_gnn_bb)])[None],
    }
    arrays = {k: np.ascontiguousarray(v) for k, v in arrays.items()}
    nc = bacc.Bacc("TRN2", target_bir_lowering=False, num_devices=1)
    args = [nc.dram_tensor(k, v.shape, mb.dt.from_np(v.dtype), kind="ExternalInput").ap() for k, v in arrays.items()]
    args.append(nc.dram_tensor("out", _OUT, mb.dt.float32, kind="ExternalOutput").ap())
    two_layer_gnn(nc, *args)
    r = run_bass_kernel_spmd(nc, [arrays], core_ids=[0])
    return r.results[0]["out"]
```

```python
import concourse.bass as bass
from concourse import mybir
from contextlib import ExitStack

P = 128


def two_layer_gnn(nc, x, adj, adj_t, w_cat, a_sa, bias_row, out):
    F32, F32R, BF16, I8 = mybir.dt.float32, mybir.dt.float32r, mybir.dt.bfloat16, mybir.dt.int8
    ALU, ACT = mybir.AluOpType, mybir.ActivationFunctionType

    N, D = x.shape
    NB = N // P
    NQ = 4
    QT = NB // NQ
    QC = QT * P
    HALF = N // 2
    KT = D // P
    HC = D + 4
    EC = D + 2
    GC = D + 2
    WC = HC + GC
    PARTS = 3
    LO_ROW = 32
    SK = 2 * PARTS
    LN_EPS, COUNT_EPS, SUM_EPS, SLOPE = 1e-5, 1e-24, 1e-5, 0.01

    ctx = ExitStack()
    with ctx:
        def sb(name, shape, dt, stack=None):
            return (stack or ctx).enter_context(nc.sbuf_tensor(name, shape, dt))

        def bank(name):
            return ctx.enter_context(nc.psum_tensor(name, [P, 512], F32))

        def sem(name):
            return ctx.enter_context(nc.semaphore(name))

        h_hi, h_lo = sb("h_hi", [P, NB, EC], F32R), sb("h_lo", [P, NB, EC], F32R)
        g_hi, g_lo = sb("g_hi", [P, NB, GC], F32R), sb("g_lo", [P, NB, GC], F32R)
        x1 = sb("x1", [P, NB, D], F32)
        blk_hi, blk_lo = sb("blk_hi", [P, NB, P], F32R), sb("blk_lo", [P, NB, P], F32R)
        cols = sb("cols", [P, 2, N], F32)
        w_f = sb("w_f", [P, KT, WC], F32)
        w_hi, w_lo = sb("w_hi", [P, KT, WC], F32R), sb("w_lo", [P, KT, WC], F32R)
        a_bc = sb("a_bc", [P, 2 * D], F32)
        xt_hi, xt_lo = sb("xt_hi", [P, KT, P], F32R), sb("xt_lo", [P, KT, P], F32R)
        brow = sb("brow", [P, GC], F32)
        brow_parts = sb("brow_parts", [P, GC], F32R)
        two_rows = sb("two_rows", [P, P], F32R)
        ident, ident_bf = sb("ident", [P, P], F32), sb("ident_bf", [P, P], BF16)
        nodecols = sb("nodecols", [P, NB, 4], F32)
        pack = sb("pack", [P, 2 * SK], BF16)
        rest1, rest2 = sb("rest1", [P, 2], F32), sb("rest2", [P, 2], F32)
        score_rows = sb("score_rows", [P, NB, 2, P], BF16)
        minus_half = sb("minus_half", [P, 1], F32)
        plus_half = sb("plus_half", [P, D], F32)
        cnt, cnt2 = sb("cnt", [P, 1], F32), sb("cnt2", [P, 2], F32)
        cnt_g = sb("cnt_g", [P, 1], F32)
        scale = sb("scale", [P, 1], F32)
        deg2 = sb("deg2", [P, 2], F32)
        deg = sb("deg", [P, 1], F32)
        rdeg = sb("rdeg", [P, 2], F32)
        stats, mv = sb("stats", [P, 6], F32), sb("mv", [P, 2], F32)
        var_g, rstd = sb("var_g", [P, 1], F32), sb("rstd", [P, 1], F32)
        y = sb("y", [P, D], F32)
        x1_now = sb("x1_now", [P, D], F32)
        one = ExitStack()
        rows = sb("rows", [P, 2, N], F32, one)
        x_hi, x_lo = sb("x_hi", [P, NB, D], F32R, one), sb("x_lo", [P, NB, D], F32R, one)
        inc = sb("inc", [P, N], F32, one)
        sgn, pos = sb("sgn", [P, N], I8, one), sb("pos", [P, N], I8, one)
        one.close()
        e = sb("e", [P, N], F32)
        e_steep = sb("e_steep", [P, 2, QC], F32)
        sb("unused", [P, N - 2 * QC], F32)
        ct_hi, ct_lo = sb("ct_hi", [P, NB, P], F32R), sb("ct_lo", [P, NB, P], F32R)
        out_sb = sb("out_sb", [P, 2, D], F32)
        nb_part = sb("nb_part", [P, D], F32)
        z, th = sb("z", [P, D], F32), sb("th", [P, D], F32)
        rrow, recip = sb("rrow", [P, 1], F32), sb("recip", [P, 1], F32)
        zl, tl, attn = sb("zl", [P, 2], F32), sb("tl", [P, 2], F32), sb("attn", [P, 2], F32)
        coef = sb("coef", [P, 1], F32)

        turned = [bank("turned0"), bank("turned1")]
        acc = [bank("acc0"), bank("acc1")]
        ps_x, ps_h, ps_g, ps_r = bank("ps_x"), bank("ps_h"), bank("ps_g"), bank("ps_r")

        def score_bank(b, q):
            return turned[q % 2] if isinstance(b, int) and b == 0 else (turned + [ps_x, ps_h])[q]

        rows_in = sem("rows_in")
        cols_in = sem("cols_in")
        half_in, half_counted = sem("half_in"), sem("half_counted")
        x_in = [sem(f"x_in{q}") for q in range(NQ)]
        w_in, a_in, b_in = sem("w_in"), sem("a_in"), sem("b_in")
        id0, id1, id_bf = sem("id0"), sem("id1"), sem("id_bf")
        ones0, ones1, pads_set = sem("ones0"), sem("ones1"), sem("pads_set")
        halves_set, brow0 = sem("halves_set"), sem("brow0")
        xhi_done, xlo_done = sem("xhi_done"), sem("xlo_done")
        sgn_done, cnt_done = sem("sgn_done"), sem("cnt_done")
        cntg_done, scale_done = sem("cntg_done"), sem("scale_done")
        inc_done = sem("inc_done")
        deg_done, rdeg_done = sem("deg_done"), sem("rdeg_done")
        turn_done = sem("turn_done")
        hi_done, lo_done = sem("hi_done"), sem("lo_done")
        acc_done, y_done = sem("acc_done"), sem("y_done")
        xq_used = sem("xq_used")
        st_done, mv_done = sem("st_done"), sem("mv_done")
        varg_done, rstd_done = sem("varg_done"), sem("rstd_done")
        x1n_done, x1_kept = sem("x1n_done"), sem("x1_kept")
        xt_done, xthi_done, xtlo_done = sem("xt_done"), sem("xthi_done"), sem("xtlo_done")
        h_done, g_done, r_done = sem("h_done"), sem("g_done"), sem("r_done")
        hhi_done, hlo_done = sem("hhi_done"), sem("hlo_done")
        ghi_done, glo_done = sem("ghi_done"), sem("glo_done")
        nodecols_done, pack_done = sem("nodecols_done"), sem("pack_done")
        rows_done = sem("rows_done")
        product_done, v_done, whi_done, wlo_done = sem("product_done"), sem("v_done"), sem("whi_done"), sem("wlo_done")
        bhi_done, blo_done = sem("bhi_done"), sem("blo_done")
        score_done, mask_done = sem("score_done"), sem("mask_done")
        flat_done, steep_done, lesser_done = sem("flat_done"), sem("steep_done"), sem("lesser_done")
        ehi_done, elo_done, eq_used = sem("ehi_done"), sem("elo_done"), sem("eq_used")
        cthi_done, ctlo_done, ctq_used = sem("cthi_done"), sem("ctlo_done"), sem("ctq_used")
        ag_done = sem("ag_done")
        zl_done, tl_done, attn_done = sem("zl_done"), sem("tl_done"), sem("attn_done")
        rrow_done, recip_done, coef_done = sem("rrow_done"), sem("recip_done"), sem("coef_done")
        nbp_done, z_done, th_done = sem("nbp_done"), sem("z_done"), sem("th_done")
        y2_done, out_done, out_stored = sem("y2_done"), sem("out_done"), sem("out_stored")

        products = cols[:, 0, 0:2 * KT * D].rearrange("p (i d) -> p i d", d=D)

        sp_waits, act_waits, pool_waits, dve_waits, pe_waits = (
            sem("sp_waits"), sem("act_waits"), sem("pool_waits"), sem("dve_waits"), sem("pe_waits"))

        block = ctx.enter_context(nc.Block())

        def once(eng, s, value):
            if not isinstance(value, int) or value > 0:
                eng.wait_ge(s, value)

        def steps(eng, step, first, last):
            lo, hi = 4, NB - 2

            def has(b):
                return {k: 0 <= b - k < NB for k in range(-2, 4)}

            for b in range(first, lo):
                step(b, b % 2, has(b))
            with eng.Fori(lo // 2, hi // 2) as t:
                for s in range(2):
                    step(2 * t + s, s, has(lo))
            for b in range(hi, last + 1):
                step(b, b % 2, has(b))

        def steps2(eng, step):
            step(0, 0, True, False)
            step(1, 1, False, False)
            with eng.Fori(1, NB // 2 - 1) as t:
                for s in range(2):
                    step(2 * t + s, s, False, False)
            step(NB - 2, 0, False, False)
            step(NB - 1, 1, False, True)

        def quarter(t, q):
            return t[:, q * QC:(q + 1) * QC]

        def tiles(t, q):
            return t[:, q * QT:(q + 1) * QT, :].rearrange("p t c -> p (t c)")

        @block.sync
        def _(sp):
            adj_b = adj.rearrange("(b p) n -> b p n", p=P)
            x_v = x.rearrange("(t p) d -> p t d", p=P)
            out_b = out.rearrange("(b p) d -> b p d", p=P)

            def load_x(q):
                sp.dma_start(x1[:, q * QT:(q + 1) * QT, :], x_v[:, q * QT:(q + 1) * QT, :]).then_inc(x_in[q], 16)

            sp.dma_start(rows[:, 0, 0:HALF], adj_b[0][:, 0:HALF]).then_inc(half_in, 16)
            sp.dma_start(rows[:, 0, HALF:N], adj_b[0][:, HALF:N]).then_inc(rows_in, 16)
            load_x(0)
            sp.wait_ge(rows_in, 16)
            sp.dma_start(rows[:, 1, :], adj_b[1]).then_inc(rows_in, 16)
            for q in range(1, NQ):
                load_x(q)
            sp.wait_ge(rows_in, 32)
            sp.wait_ge(inc_done, 2)
            sp.dma_start(rows[:, 0, :], adj_b[2]).then_inc(rows_in, 16)
            sp.dma_start(w_f[:, :, :], w_cat.rearrange("(k p) c -> p k c", p=P)).then_inc(w_in, 16)
            sp.dma_start(a_bc[:, :], a_sa.partition_broadcast(P)).then_inc(a_in, 16)
            sp.wait_ge(brow0, 1)
            for r in (0, LO_ROW):
                sp.dma_start(brow[r:r + 1, :], bias_row).then_inc(b_in, 16)
            sp.wait_ge(rows_in, 48)
            sp.wait_ge(inc_done, 4)
            sp.dma_start(rows[:, 1, :], adj_b[3]).then_inc(rows_in, 16)
            with sp.Fori(2, NB // 2) as t:
                for s in range(2):
                    b = 2 * t + s
                    sp.wait_ge(rows_in, 16 * b)
                    sp.sem_inc(sp_waits, 1)
                    sp.wait_ge(inc_done, 2 * (b - 2) + 2)
                    sp.sem_inc(sp_waits, 1)
                    sp.dma_start(rows[:, s, :], adj_b[b]).then_inc(rows_in, 16)
            sp.wait_ge(v_done, 2 * KT)
            sp.dma_start(cols[:, 0, :], adj_t[0]).then_inc(cols_in, 16)
            sp.wait_ge(cols_in, 16)
            sp.dma_start(cols[:, 1, :], adj_t[1]).then_inc(cols_in, 16)

            def load(b, s):
                sp.wait_ge(cols_in, 16 * b)
                sp.sem_inc(sp_waits, 1)
                sp.wait_ge(ctlo_done, NQ * (b - 2) + NQ)
                sp.sem_inc(sp_waits, 1)
                sp.wait_ge(mask_done, NQ * (b - 2) + NQ)
                sp.sem_inc(sp_waits, 1)
                sp.dma_start(cols[:, s, :], adj_t[b]).then_inc(cols_in, 16)

            def store(b, s, first=False):
                if not first:
                    sp.wait_ge(out_stored, 16 * b)
                    sp.sem_inc(sp_waits, 1)
                sp.wait_ge(out_done, b + 1)
                sp.sem_inc(sp_waits, 1)
                sp.dma_start(out_b[b], out_sb[:, s, :]).then_inc(out_stored, 16)

            LAG = 4
            for b in range(2, LAG + 2):
                load(b, b % 2)
                if b >= LAG:
                    store(b - LAG, b % 2, first=b == LAG)
            with sp.Fori(LAG // 2 + 1, NB // 2) as t:
                for s in range(2):
                    load(2 * t + s, s)
                    store(2 * t + s - LAG, s)
            for b in range(NB - LAG, NB):
                store(b, b % 2)
            sp.wait_ge(out_stored, 16 * NB)

        @block.gpsimd
        def _(pool):
            pool.memset(ident[:, :], 0.0).then_inc(id0, 1)
            pool.memset(minus_half[:, :], -0.5).then_inc(halves_set, 1)
            pool.memset(plus_half[:, :], 0.5).then_inc(halves_set, 1)
            pool.memset(two_rows[:, :].bitcast(F32), 0.0).then_inc(ones0, 1)
            pool.memset(brow[:, :], 0.0).then_inc(brow0, 1)
            pool.wait_ge(id0, 1)
            pool.affine_select(out=ident[:, :], in_=ident[:, :], compare_op=ALU.not_equal, fill=1.0, base=0,
                               pattern=[[-1, P]], channel_multiplier=1).then_inc(id1, 1)
            pool.wait_ge(ones0, 1)
            pool.memset(two_rows[0:1, :].bitcast(F32), 1.0).then_inc(ones1, 1)
            pool.memset(pack[:, :], 1.0).then_inc(pads_set, 1)
            pool.memset(h_hi[:, :, D:D + 1].bitcast(F32), 1.0).then_inc(pads_set, 1)
            pool.memset(h_hi[:, :, D + 1:D + 2].bitcast(F32), 0.0).then_inc(pads_set, 1)
            pool.memset(h_lo[:, :, D:D + 2].bitcast(F32), 0.0).then_inc(pads_set, 1)
            pool.wait_ge(id1, 1)
            pool.wait_ge(pads_set, 4)
            pool.memset(two_rows[LO_ROW:LO_ROW + 1, :].bitcast(F32), 1.0).then_inc(ones1, 1)
            pool.wait_ge(ones1, 2)
            pool.tensor_copy(ident_bf[:, :], ident[:, :]).then_inc(id_bf, 1)
            pool.wait_ge(halves_set, 2)

            def rsqrt_of_var(n, phase1):
                once(pool, rstd_done, n)
                pool.wait_ge(mv_done, n + 1)
                pool.sem_inc(pool_waits, 1)
                pool.tensor_scalar(var_g[:, :], mv[:, 1:2], LN_EPS, 1.0, ALU.add, ALU.mult).then_inc(varg_done, 1)
                pool.wait_ge(varg_done, n + 1)
                once(pool, x1n_done, n if phase1 else NB)
                if not phase1:
                    once(pool, out_done, n - NB)
                pool.tensor_tensor(rstd[:, :], var_g[:, :], minus_half[:, :], ALU.pow).then_inc(rstd_done, 1)

            def parts_of_scores(b):
                def part(k):
                    return pack[:, PARTS + k:2 * PARTS + k + 1:PARTS]

                once(pool, r_done, b)
                pool.wait_ge(nodecols_done, b + 1)
                pool.sem_inc(pool_waits, 1)
                pool.tensor_copy(part(0), nodecols[:, b, 0:2]).then_inc(pack_done, 1)
                pool.wait_ge(pack_done, 5 * b + 1)
                pool.sem_inc(pool_waits, 1)
                pool.tensor_tensor(rest1[:, :], nodecols[:, b, 0:2], part(0), ALU.subtract).then_inc(pack_done, 1)
                pool.wait_ge(pack_done, 5 * b + 2)
                pool.sem_inc(pool_waits, 1)
                pool.tensor_copy(part(1), rest1[:, :]).then_inc(pack_done, 1)
                pool.wait_ge(pack_done, 5 * b + 3)
                pool.sem_inc(pool_waits, 1)
                pool.tensor_tensor(rest2[:, :], rest1[:, :], part(1), ALU.subtract).then_inc(pack_done, 1)
                pool.wait_ge(pack_done, 5 * b + 4)
                pool.sem_inc(pool_waits, 1)
                pool.tensor_copy(part(2), rest2[:, :]).then_inc(pack_done, 1)

            def keep_x1(b):
                pool.wait_ge(x1n_done, b + 1)
                pool.sem_inc(pool_waits, 1)
                pool.tensor_tensor(x1[:, b, :], x1_now[:, :], plus_half[:, :], ALU.add).then_inc(x1_kept, 1)

            def x_to_lo(q):
                pool.wait_ge(xhi_done, q + 1)
                t = slice(q * QT, (q + 1) * QT)
                pool.tensor_tensor(x_lo[:, t, :], x1[:, t, :], x_hi[:, t, :].bitcast(F32), ALU.subtract).then_inc(xlo_done, 1)

            def step(b, s, has):
                if has[1]:
                    rsqrt_of_var(b - 1, True)
                if has[-2]:
                    once(pool, scale_done, b + 2)
                    pool.wait_ge(cnt_done, b + 3)
                    pool.sem_inc(pool_waits, 1)
                    pool.tensor_scalar(cnt_g[:, :], cnt[:, :], float(2 * N), COUNT_EPS, ALU.min, ALU.max).then_inc(cntg_done, 1)
                    pool.wait_ge(cntg_done, b + 3)
                    once(pool, inc_done, 2 * (b + 1) + 2 if not isinstance(b, int) or b > -2 else 0)
                    pool.tensor_tensor(scale[:, :], cnt_g[:, :], minus_half[:, :], ALU.pow).then_inc(scale_done, 1)
                if isinstance(b, int) and b < 0:
                    x_to_lo(b + 2)
                if isinstance(b, int) and b == 0:
                    pool.wait_ge(w_in, 16)
                    pool.wait_ge(a_in, 16)
                    for k in range(KT):
                        for i in range(2):
                            pool.tensor_tensor(products[:, 2 * k + i, :], w_f[:, k, 0:D],
                                               a_bc[:, i * D:(i + 1) * D], ALU.mult).then_inc(product_done, 1)
                if has[1]:
                    keep_x1(b - 1)
                if isinstance(b, int) and b == 1:
                    pool.wait_ge(whi_done, 1)
                    pool.tensor_tensor(w_lo[:, :, :], w_f[:, :, :], w_hi[:, :, :].bitcast(F32), ALU.subtract).then_inc(wlo_done, 1)
                if has[2]:
                    parts_of_scores(b - 2)

            steps(pool, step, -2, NB - 1)

            def cols_lo(b, s, q):
                pool.wait_ge(cthi_done, NQ * b + q + 1)
                pool.sem_inc(pool_waits, 1)
                if isinstance(b, int) and b == 0:
                    pool.wait_ge(xq_used, NQ // 2 + q // 2 + 1)
                    once(pool, ctlo_done, q)
                pool.tensor_tensor(tiles(ct_lo, q), quarter(cols[:, s, :], q), tiles(ct_hi, q).bitcast(F32),
                                   ALU.subtract).then_inc(ctlo_done, 1)

            L = NB - 1
            cols_lo(0, 0, 0)
            rsqrt_of_var(L, True)
            keep_x1(L)
            parts_of_scores(L - 1)
            cols_lo(0, 0, 2)
            parts_of_scores(L)

            def step2(b, s, first, last):
                if not first:
                    rsqrt_of_var(NB + b - 1, False)
                if not last:
                    for q in range(NQ):
                        cols_lo(b + 1, 1 - s, q)

            steps2(pool, step2)
            rsqrt_of_var(2 * NB - 1, False)

        @block.scalar
        def _(act):
            def split_hi(n, q):
                act.wait_ge(turn_done, n + 1)
                nc.scalar.copy(tiles(blk_hi, q), turned[q % 2][:, :]).then_inc(hi_done, 1)

            def signs(b, s):
                act.wait_ge(rows_in, 16 * (b + 1))
                once(act, cnt_done, b)
                nc.scalar.activation(sgn[:, :], rows[:, s, :], ACT.Sign).then_inc(sgn_done, 1)

            def positives(b):
                act.wait_ge(sgn_done, b - 1)
                act.wait_ge(inc_done, 2 * b)
                act.wait_ge(cntg_done, b)
                nc.scalar.activation(pos[:, :], sgn[:, :], ACT.Relu, accum_out=cnt[:, :]).then_inc(cnt_done, 1)

            def x_to_hi(q):
                act.wait_ge(x_in[q], 16)
                nc.scalar.copy(x_hi[:, q * QT:(q + 1) * QT, :], x1[:, q * QT:(q + 1) * QT, :]).then_inc(xhi_done, 1)

            def turned_x1_hi(b):
                act.wait_ge(xt_done, b + 1)
                nc.scalar.copy(xt_hi[:, :, :].rearrange("p k c -> p (k c)"), ps_x[:, 0:D]).then_inc(xthi_done, 1)

            def h_to_hi(b):
                act.wait_ge(h_done, b + 1)
                act.sem_inc(act_waits, 1)
                nc.scalar.copy(h_hi[:, b, 0:D], ps_h[:, 0:D]).then_inc(hhi_done, 1)

            def g_to_hi(b):
                act.wait_ge(g_done, b + 1)
                act.sem_inc(act_waits, 1)
                nc.scalar.copy(g_hi[:, b, :], ps_g[:, 0:GC]).then_inc(ghi_done, 1)

            def rows_of_scores(b):
                act.wait_ge(r_done, b + 1)
                act.sem_inc(act_waits, 1)
                nc.scalar.copy(score_rows[0:SK, b, :, :].rearrange("p i c -> p (i c)"), ps_r[0:SK, 0:2 * P]).then_inc(rows_done, 1)

            def step(b, s, has):
                if isinstance(b, int) and b == -2:
                    x_to_hi(0)
                    return
                if isinstance(b, int) and b == 0:
                    signs(2, 0)
                for q in range(NQ):
                    if has[2] and q == 0:
                        turned_x1_hi(b - 2)
                    if has[-1]:
                        split_hi(NQ * (b + 1) + q, q)
                    if has[-2] and q == 0 and not (isinstance(b, int) and b <= 0):
                        signs(b + 2, s)
                    if has[-2] and q == (0 if isinstance(b, int) and b == 0 else 1) and not (isinstance(b, int) and b < 0):
                        positives(b + 2)
                    if isinstance(b, int) and b == -1 and q > 0:
                        x_to_hi(q)
                    if isinstance(b, int) and b == 0 and q == 3:
                        for k in range(KT):
                            for i in range(2):
                                act.wait_ge(product_done, 2 * k + i + 1)
                                v = products[:, 2 * k + i, :]
                                nc.scalar.activation(v, v, ACT.Copy, accum_out=w_f[:, k, D + i:D + i + 1]).then_inc(v_done, 1)
                    if isinstance(b, int) and b == 1 and q == 3:
                        act.wait_ge(v_done, 2 * KT)
                        nc.scalar.copy(w_hi[:, :, :], w_f[:, :, :]).then_inc(whi_done, 1)
                        act.wait_ge(b_in, 32)
                        nc.scalar.copy(brow_parts[:, :], brow[:, :]).then_inc(bhi_done, 1)
                    if has[2] and q == 2:
                        h_to_hi(b - 2)
                    if has[2] and q == 3:
                        g_to_hi(b - 2)
                    if has[3] and q == 2:
                        rows_of_scores(b - 3)

            steps(act, step, -2, NB - 2)

            def exps(b, q):
                act.wait_ge(score_done, NQ * b + q + 1)
                if isinstance(b, int) and b == 0:
                    act.wait_ge(inc_done, 2 * NB)
                else:
                    act.wait_ge(elo_done, NQ * (b - 1) + q + 1)
                nc.scalar.activation(quarter(e, q), score_bank(b, q)[:, :], ACT.Exp, scale=-SLOPE).then_inc(flat_done, 1)
                if not isinstance(b, int) or b > 0 or q > 1:
                    act.wait_ge(lesser_done, NQ * b + q - 1)
                nc.scalar.activation(e_steep[:, q % 2, :], score_bank(b, q)[:, :], ACT.Exp, scale=-1.0).then_inc(steep_done, 1)

            def e_hi(b, q):
                act.wait_ge(mask_done, NQ * b + q + 1)
                if isinstance(b, int) and b == 0:
                    act.wait_ge(xq_used, NQ)
                else:
                    act.wait_ge(eq_used, NQ * (b - 1) + q + 1)
                nc.scalar.copy(tiles(blk_hi, q), quarter(e, q)).then_inc(ehi_done, 1)

            def cols_hi(b, s, q):
                if q == 0:
                    act.wait_ge(cols_in, 16 * (b + 1))
                if isinstance(b, int) and b == 0:
                    act.wait_ge(xq_used, q // 2 + 1)
                else:
                    act.wait_ge(ctq_used, NQ * (b - 1) + q + 1)
                nc.scalar.copy(tiles(ct_hi, q), quarter(cols[:, s, :], q)).then_inc(cthi_done, 1)

            def gates(b):
                once(act, attn_done, b)
                act.wait_ge(zl_done, b + 1)
                nc.scalar.activation(tl[:, :], zl[:, :], ACT.Tanh, scale=0.5).then_inc(tl_done, 1)

            def neighbours(b):
                once(act, z_done, b)
                act.wait_ge(attn_done, b + 1)
                nc.scalar.activation(nb_part[:, :], acc[1][:, 0:D], ACT.Copy, scale=attn[:, 1:2]).then_inc(nbp_done, 1)

            def final(b):
                once(act, y2_done, b)
                act.wait_ge(z_done, b + 1)
                nc.scalar.activation(th[:, :], z[:, :], ACT.Tanh, scale=0.5).then_inc(th_done, 1)

            L = NB - 1
            turned_x1_hi(L - 2)
            rows_of_scores(L - 3)
            exps(0, 0)
            h_to_hi(L - 2)
            g_to_hi(L - 2)
            cols_hi(0, 0, 0)
            turned_x1_hi(L - 1)
            cols_hi(0, 0, 1)
            rows_of_scores(L - 2)
            exps(0, 1)
            h_to_hi(L - 1)
            exps(0, 2)
            g_to_hi(L - 1)
            cols_hi(0, 0, 2)
            turned_x1_hi(L)
            e_hi(0, 0)
            h_to_hi(L)
            cols_hi(0, 0, 3)
            g_to_hi(L)
            rows_of_scores(L - 1)
            e_hi(0, 1)
            rows_of_scores(L)
            e_hi(0, 2)
            exps(0, 3)
            cols_hi(1, 1, 0)
            e_hi(0, 3)

            def step2(b, s, first, last):
                s1 = 1 - s
                if not first:
                    e_hi(b, 0)
                    e_hi(b, 1)
                    e_hi(b, 2)
                    final(b - 1)
                    if not last:
                        cols_hi(b + 1, s1, 0)
                    e_hi(b, 3)
                    if not last:
                        cols_hi(b + 1, s1, 1)
                if last:
                    gates(b)
                    neighbours(b)
                else:
                    exps(b + 1, 0)
                    if first:
                        cols_hi(b + 1, s1, 1)
                    gates(b)
                    cols_hi(b + 1, s1, 2)
                    neighbours(b)
                    exps(b + 1, 1)
                    cols_hi(b + 1, s1, 3)
                    exps(b + 1, 2)
                    exps(b + 1, 3)

            steps2(act, step2)
            final(NB - 1)

        @block.vector
        def _(dve):
            def split_lo(n, q):
                dve.wait_ge(hi_done, n + 1)
                nc.vector.tensor_tensor(tiles(blk_lo, q), turned[q % 2][:, :], tiles(blk_hi, q).bitcast(F32),
                                        ALU.subtract).then_inc(lo_done, 1)

            def build_inc(b, s, half):
                if half == 0:
                    dve.wait_ge(scale_done, b + 1)
                if not isinstance(b, int) or b > 0:
                    dve.wait_ge(turn_done, NQ * (b - 1) + 2 * half + 2)
                    if half == 0:
                        dve.wait_ge(deg_done, b)
                c = slice(half * HALF, (half + 1) * HALF)
                nc.vector.scalar_tensor_tensor(out=inc[:, c], in0=pos[:, c], scalar=scale[:, :], in1=rows[:, s, c],
                                               op0=ALU.mult, op1=ALU.add, accum_out=deg2[:, half:half + 1]).then_inc(inc_done, 1)

            def layer_norm_stats(n):
                once(dve, mv_done, n)
                nc.vector.bn_stats(stats[:, :], y[:, :]).then_inc(st_done, 1)

            def layer_norm_moments(n):
                once(dve, varg_done, n)
                dve.wait_ge(st_done, n + 1)
                dve.sem_inc(dve_waits, 1)
                nc.vector.bn_aggr(mv[:, :], stats[:, :]).then_inc(mv_done, 1)

            def x_to_lo(q):
                dve.wait_ge(xhi_done, q + 1)
                dve.wait_ge(xlo_done, q)
                t = slice(q * QT, (q + 1) * QT)
                nc.vector.tensor_tensor(x_lo[:, t, :], x1[:, t, :], x_hi[:, t, :].bitcast(F32),
                                        ALU.subtract).then_inc(xlo_done, 1)

            def residual(b, s):
                once(dve, x1n_done, b)
                dve.wait_ge(rdeg_done, b + 1)
                if isinstance(b, int) and b == NB - 1:
                    dve.wait_ge(xq_used, NQ)
                else:
                    dve.wait_ge(acc_done, b + 1)
                nc.vector.scalar_tensor_tensor(out=y[:, :], in0=acc[s][:, 0:D], scalar=rdeg[:, s:s + 1],
                                               in1=x1[:, b, :], op0=ALU.mult, op1=ALU.add).then_inc(y_done, 1)

            def turned_x1_lo(b):
                dve.wait_ge(xthi_done, b + 1)
                nc.vector.tensor_tensor(xt_lo[:, :, :].rearrange("p k c -> p (k c)"), ps_x[:, 0:D],
                                        xt_hi[:, :, :].rearrange("p k c -> p (k c)").bitcast(F32),
                                        ALU.subtract).then_inc(xtlo_done, 1)

            def normed(b):
                dve.wait_ge(rstd_done, b + 1)
                once(dve, xt_done, b)
                once(dve, x1_kept, b)
                nc.vector.tensor_scalar(x1_now[:, :], y[:, :], mv[:, 0:1], rstd[:, :], ALU.subtract,
                                        ALU.mult).then_inc(x1n_done, 1)

            def h_rest(b):
                dve.wait_ge(hhi_done, b + 1)
                nc.vector.tensor_copy(nodecols[:, b, :], ps_h[:, D:HC]).then_inc(nodecols_done, 1)
                nc.vector.tensor_tensor(h_lo[:, b, 0:D], ps_h[:, 0:D], h_hi[:, b, 0:D].bitcast(F32),
                                        ALU.subtract).then_inc(hlo_done, 1)

            def g_rest(b):
                dve.wait_ge(ghi_done, b + 1)
                nc.vector.tensor_tensor(g_lo[:, b, :], ps_g[:, 0:GC], g_hi[:, b, :].bitcast(F32),
                                        ALU.subtract).then_inc(glo_done, 1)

            def first_positives(b, halves):
                if b == 1 and halves[0] == 0:
                    dve.wait_ge(inc_done, 2)
                    dve.wait_ge(cnt_done, 1)
                    dve.wait_ge(cntg_done, 1)
                for half in halves:
                    if b == 0 and half == 0:
                        dve.wait_ge(half_in, 16)
                    else:
                        dve.wait_ge(rows_in, 16 * (b + 1))
                    c = slice(half * HALF, (half + 1) * HALF)
                    nc.vector.tensor_scalar(pos[:, c], rows[:, b, c], 0.0, None, ALU.is_gt, ALU.add,
                                            accum_out=cnt2[:, half:half + 1]).then_inc(half_counted, 1)
                if 1 in halves:
                    dve.wait_ge(half_counted, 2 * b + 2)
                    nc.vector.tensor_tensor(cnt[:, :], cnt2[:, 0:1], cnt2[:, 1:2], ALU.add).then_inc(cnt_done, 1)

            def step(b, s, has):
                if isinstance(b, int) and b == -2:
                    first_positives(0, (0, 1))
                if has[1]:
                    residual(b - 1, 1 - s)
                if has[2]:
                    turned_x1_lo(b - 2)
                if has[1]:
                    dve.wait_ge(y_done, b)
                    layer_norm_stats(b - 1)
                    layer_norm_moments(b - 1)
                if has[-1]:
                    build_inc(b + 1, 1 - s, 1)
                if isinstance(b, int) and b == -1:
                    first_positives(1, (0,))
                if has[-1]:
                    split_lo(NQ * (b + 1), 0)
                if isinstance(b, int) and b == -1:
                    first_positives(1, (1,))
                if has[-1]:
                    dve.wait_ge(inc_done, 2 * (b + 1) + 2)
                    once(dve, rdeg_done, b + 1)
                    nc.vector.tensor_tensor(deg[:, :], deg2[:, 0:1], deg2[:, 1:2], ALU.add).then_inc(deg_done, 1)
                if isinstance(b, int) and b == 0:
                    x_to_lo(3)
                if has[-1]:
                    once(dve, y_done, b)
                    dve.wait_ge(deg_done, b + 2)
                    nc.vector.reciprocal(rdeg[:, 1 - s:2 - s], deg[:, :]).then_inc(rdeg_done, 1)
                    split_lo(NQ * (b + 1) + 1, 1)
                if has[1]:
                    normed(b - 1)
                if has[-1]:
                    split_lo(NQ * (b + 1) + 2, 2)
                if has[-2]:
                    build_inc(b + 2, s, 0)
                if has[2]:
                    h_rest(b - 2)
                if has[-1]:
                    split_lo(NQ * (b + 1) + 3, 3)
                if has[2]:
                    g_rest(b - 2)
                if isinstance(b, int) and b == 2:
                    dve.wait_ge(bhi_done, 1)
                    lo = slice(LO_ROW, LO_ROW + 1)
                    nc.vector.tensor_tensor(brow_parts[lo, :], brow[lo, :], brow_parts[lo, :].bitcast(F32),
                                            ALU.subtract).then_inc(blo_done, 1)
                if isinstance(b, int) and b == -1:
                    x_to_lo(2)

            steps(dve, step, -2, NB - 2)

            def lesser(b, q):
                dve.wait_ge(flat_done, NQ * b + q + 1)
                dve.wait_ge(steep_done, NQ * b + q + 1)
                nc.vector.tensor_tensor(quarter(e, q), quarter(e, q), e_steep[:, q % 2, :], ALU.min).then_inc(lesser_done, 1)

            def mask(b, s, q):
                dve.wait_ge(lesser_done, NQ * b + q + 1)
                if q == 0:
                    dve.wait_ge(cols_in, 16 * (b + 1))
                nc.vector.scalar_tensor_tensor(out=quarter(e, q), in0=quarter(cols[:, s, :], q), scalar=0.0,
                                               in1=quarter(e, q), op0=ALU.not_equal, op1=ALU.mult).then_inc(mask_done, 1)

            def e_lo(b, q):
                dve.wait_ge(ehi_done, NQ * b + q + 1)
                nc.vector.tensor_tensor(tiles(blk_lo, q), quarter(e, q), tiles(blk_hi, q).bitcast(F32),
                                        ALU.subtract).then_inc(elo_done, 1)

            def first_cols_lo(q):
                dve.wait_ge(ctlo_done, q)
                dve.wait_ge(cthi_done, q + 1)
                dve.wait_ge(xq_used, NQ // 2 + q // 2 + 1)
                nc.vector.tensor_tensor(tiles(ct_lo, q), quarter(cols[:, 0, :], q), tiles(ct_hi, q).bitcast(F32),
                                        ALU.subtract).then_inc(ctlo_done, 1)

            def logits(b):
                once(dve, tl_done, b)
                dve.wait_ge(ag_done, b + 1)
                nc.vector.tensor_tensor(zl[:, :], acc[1][:, D:D + 2], nodecols[:, b, 2:4], ALU.add).then_inc(zl_done, 1)

            def attention(b):
                once(dve, coef_done, b)
                once(dve, nbp_done, b)
                dve.wait_ge(tl_done, b + 1)
                nc.vector.tensor_scalar(attn[:, :], tl[:, :], 0.5, 0.5, ALU.mult, ALU.add).then_inc(attn_done, 1)

            def rowsum(b):
                once(dve, recip_done, b)
                dve.wait_ge(eq_used, NQ * b + NQ)
                nc.vector.tensor_scalar(rrow[:, :], acc[0][:, D:D + 1], SUM_EPS, None, ALU.add).then_inc(rrow_done, 1)

            def reciprocal(b):
                dve.wait_ge(rrow_done, b + 1)
                once(dve, coef_done, b)
                nc.vector.reciprocal(recip[:, :], rrow[:, :]).then_inc(recip_done, 1)

            def coefficient(b):
                dve.wait_ge(recip_done, b + 1)
                once(dve, z_done, b)
                nc.vector.tensor_tensor(coef[:, :], recip[:, :], attn[:, 0:1], ALU.mult).then_inc(coef_done, 1)

            def combine(b):
                once(dve, th_done, b)
                dve.wait_ge(nbp_done, b + 1)
                dve.wait_ge(coef_done, b + 1)
                nc.vector.scalar_tensor_tensor(out=z[:, :], in0=acc[0][:, 0:D], scalar=coef[:, :], in1=nb_part[:, :],
                                               op0=ALU.mult, op1=ALU.add).then_inc(z_done, 1)

            def sigmoid_sum(b):
                dve.wait_ge(th_done, b + 1)
                once(dve, out_done, b)
                nc.vector.scalar_tensor_tensor(out=y[:, :], in0=th[:, :], scalar=0.5, in1=x1[:, b, :],
                                               op0=ALU.mult, op1=ALU.add).then_inc(y2_done, 1)

            def finish(b, s):
                dve.wait_ge(rstd_done, NB + b + 1)
                if not isinstance(b, int) or b > 1:
                    dve.wait_ge(out_stored, 16 * (b - 1))
                nc.vector.tensor_scalar(out_sb[:, s, :], y[:, :], mv[:, 0:1], rstd[:, :], ALU.subtract,
                                        ALU.mult).then_inc(out_done, 1)

            L = NB - 1
            residual(L - 1, (L - 1) % 2)
            turned_x1_lo(L - 2)
            dve.wait_ge(y_done, L)
            layer_norm_stats(L - 1)
            layer_norm_moments(L - 1)
            lesser(0, 0)
            normed(L - 1)
            h_rest(L - 2)
            g_rest(L - 2)
            turned_x1_lo(L - 1)
            residual(L, L % 2)
            dve.wait_ge(y_done, L + 1)
            layer_norm_stats(L)
            first_cols_lo(1)
            layer_norm_moments(L)
            mask(0, 0, 0)
            lesser(0, 1)
            normed(L)
            lesser(0, 2)
            h_rest(L - 1)
            g_rest(L - 1)
            turned_x1_lo(L)
            mask(0, 0, 1)
            mask(0, 0, 2)
            e_lo(0, 0)
            h_rest(L)
            first_cols_lo(3)
            g_rest(L)
            e_lo(0, 1)
            e_lo(0, 2)
            lesser(0, 3)
            mask(0, 0, 3)
            e_lo(0, 3)

            def step2(b, s, first, last):
                s1 = 1 - s
                if not first:
                    rowsum(b - 1)
                    mask(b, s, 2)
                    reciprocal(b - 1)
                    lesser(b, 3)
                    coefficient(b - 1)
                    e_lo(b, 0)
                    combine(b - 1)
                    mask(b, s, 3)
                    e_lo(b, 1)
                    sigmoid_sum(b - 1)
                    e_lo(b, 2)
                    dve.wait_ge(y2_done, b)
                    layer_norm_stats(NB + b - 1)
                    e_lo(b, 3)
                    layer_norm_moments(NB + b - 1)
                logits(b)
                if not last:
                    lesser(b + 1, 0)
                attention(b)
                if not first:
                    finish(b - 1, s1)
                if not last:
                    mask(b + 1, s1, 0)
                    lesser(b + 1, 1)
                    mask(b + 1, s1, 1)
                    lesser(b + 1, 2)

            steps2(dve, step2)
            rowsum(L)
            reciprocal(L)
            coefficient(L)
            combine(L)
            sigmoid_sum(L)
            dve.wait_ge(y2_done, NB)
            layer_norm_stats(NB + L)
            layer_norm_moments(NB + L)
            finish(L, L % 2)

        @block.tensor
        def _(pe):
            def transpose_quarter(n, src, q):
                if not isinstance(n, int) or n >= 2:
                    pe.wait_ge(lo_done, n - 1)
                for t in range(QT):
                    last = nc.tensor.transpose(turned[q % 2][:, t * P:(t + 1) * P],
                                               src[:, (q * QT + t) * P:(q * QT + t + 1) * P], ident[:, :])
                last.then_inc(turn_done, 1)

            def three(dst, hi, lo, mv_hi, mv_lo, start, stop):
                nc.tensor.matmul(dst, hi, mv_hi, start=start, stop=False)
                nc.tensor.matmul(dst, hi, mv_lo, start=False, stop=False)
                return nc.tensor.matmul(dst, lo, mv_hi, start=False, stop=stop)

            def product_quarter(dst, a_hi, a_lo, m_hi, m_lo, q, last_stops=True):
                for t in range(q * QT, (q + 1) * QT):
                    last = three(dst, a_hi[:, t, :], a_lo[:, t, :], m_hi[:, t, :], m_lo[:, t, :],
                                 t == 0, last_stops and t == NB - 1)
                return last

            def project(dst, c0, c1):
                for k in range(KT):
                    last = three(dst, xt_hi[:, k, :], xt_lo[:, k, :], w_hi[:, k, c0:c1], w_lo[:, k, c0:c1],
                                 k == 0, k == KT - 1)
                return last

            def keep_busy(n):
                for _ in range(n):
                    nc.tensor.transpose(ps_x[:, 0:P], ident[:, :], ident[:, :])

            def projections_h(b):
                pe.wait_ge(xtlo_done, b + 1)
                if isinstance(b, int) and b == 0:
                    pe.wait_ge(wlo_done, 1)
                else:
                    pe.wait_ge(hlo_done, b)
                project(ps_h[:, 0:HC], 0, HC).then_inc(h_done, 1)

            def projections_g(b):
                once(pe, glo_done, b)
                project(ps_g[:, 0:GC], HC, WC).then_inc(g_done, 1)

            def turn_parts(b):
                once(pe, rows_done, b)
                if isinstance(b, int) and b == 0:
                    pe.wait_ge(id_bf, 1)
                pe.wait_ge(pack_done, 5 * b + 5)
                nc.tensor.matmul(ps_r[0:SK, 0:P], pack[:, 0:SK], ident_bf[:, :], start=True, stop=True)
                nc.tensor.matmul(ps_r[0:SK, P:2 * P], pack[:, SK:2 * SK], ident_bf[:, :], start=True,
                                 stop=True).then_inc(r_done, 1)

            def turn_x1(b):
                pe.wait_ge(x1n_done, b + 1)
                once(pe, xtlo_done, b)
                for k in range(KT):
                    last = nc.tensor.transpose(ps_x[:, k * P:(k + 1) * P], x1_now[:, k * P:(k + 1) * P], ident[:, :])
                last.then_inc(xt_done, 1)

            def inc_product(b, s, q):
                pe.wait_ge(lo_done, NQ * b + q + 1)
                if isinstance(b, int) and b == 0:
                    pe.wait_ge(xlo_done, q + 1)
                if q == 0 and (not isinstance(b, int) or b > 1):
                    pe.wait_ge(y_done, b - 1)
                last = product_quarter(acc[s][:, 0:D], blk_hi, blk_lo, x_hi, x_lo, q)
                if isinstance(b, int) and b == NB - 1:
                    last.then_inc(xq_used, 1)
                elif q == NQ - 1:
                    last.then_inc(acc_done, 1)

            def step(b, s, has):
                for q in range(NQ):
                    if has[0]:
                        inc_product(b, s, q)
                    if has[3] and q == 1:
                        turn_parts(b - 3)
                    if has[-1]:
                        if q % 2 == 0:
                            pe.wait_ge(inc_done, 2 * (b + 1) + q // 2 + 1)
                        transpose_quarter(NQ * (b + 1) + q, inc, q)
                        if isinstance(b, int) and b == -1 and q in (1, 2):
                            keep_busy(16)
                    if has[2] and q == 1:
                        projections_h(b - 2)
                    if has[2] and q == 2:
                        projections_g(b - 2)
                    if has[1] and q == 3:
                        turn_x1(b - 1)

            pe.wait_ge(id1, 1)
            keep_busy(44)
            steps(pe, step, -1, NB - 2)

            def scores(b, q):
                if isinstance(b, int) and b == 0:
                    pe.wait_ge(rows_done, QT * (q + 1))
                if isinstance(b, int) and b == 0 and q < 2:
                    pe.wait_ge(lo_done, NQ * NB - 1 + q)
                elif isinstance(b, int) and b == 0:
                    pe.wait_ge(steep_done, q - 1)
                elif isinstance(b, int) and b == 1:
                    if q < 2:
                        pe.wait_ge(steep_done, q + 3)
                    else:
                        pe.wait_ge((xtlo_done, hlo_done)[q - 2], NB)
                else:
                    pe.wait_ge(steep_done, NQ * (b - 1) + q + 1)
                pe.sem_inc(pe_waits, 1)
                for t in range(QT):
                    last = nc.tensor.matmul(score_bank(b, q)[:, t * P:(t + 1) * P], score_rows[0:SK, q * QT + t, 1, :],
                                            score_rows[0:SK, b, 0, :], start=True, stop=True)
                last.then_inc(score_done, 1)

            def ag_product(b, q):
                pe.wait_ge(ctlo_done, NQ * b + q + 1)
                if isinstance(b, int) and b == 0:
                    pe.wait_ge(glo_done, QT * (q + 1))
                    if q == 0:
                        pe.wait_ge(y_done, NB)
                elif q == 0:
                    pe.wait_ge(nbp_done, b)
                    pe.wait_ge(zl_done, b)
                product_quarter(acc[1][:, 0:GC], ct_hi, ct_lo, g_hi, g_lo, q, last_stops=False).then_inc(ctq_used, 1)
                if q == NQ - 1:
                    nc.tensor.matmul(acc[1][:, 0:GC], two_rows[:, :], brow_parts[:, :], start=False,
                                     stop=True).then_inc(ag_done, 1)

            def eh_product(b, q):
                pe.wait_ge(elo_done, NQ * b + q + 1)
                if isinstance(b, int) and b == 0:
                    pe.wait_ge(hlo_done, QT * (q + 1))
                    if q == 0:
                        pe.wait_ge(pads_set, 4)
                elif q == 0:
                    pe.wait_ge(z_done, b)
                last = product_quarter(acc[0][:, 0:EC], blk_hi, blk_lo, h_hi, h_lo, q)
                last.then_inc(eq_used, 1)

            L = NB - 1
            inc_product(L, L % 2, 0)
            turn_parts(L - 3)
            scores(0, 0)
            inc_product(L, L % 2, 1)
            projections_h(L - 2)
            scores(0, 1)
            inc_product(L, L % 2, 2)
            projections_g(L - 2)
            turn_x1(L - 1)
            inc_product(L, L % 2, 3)
            turn_parts(L - 2)
            scores(0, 2)
            projections_h(L - 1)
            projections_g(L - 1)
            pe.wait_ge(ones1, 2)
            pe.wait_ge(blo_done, 1)
            ag_product(0, 0)
            turn_x1(L)
            ag_product(0, 1)
            projections_h(L)
            projections_g(L)
            turn_parts(L - 1)
            ag_product(0, 2)
            turn_parts(L)
            ag_product(0, 3)

            def step2(b, s, first, last):
                if not first:
                    for q in range(NQ):
                        ag_product(b, q)
                if first:
                    scores(0, 3)
                    eh_product(b, 0)
                    eh_product(b, 1)
                if not last:
                    for q in range(NQ):
                        scores(b + 1, q)
                for q in range(2 if first else 0, NQ):
                    eh_product(b, q)

            steps2(pe, step2)


_OUT = (2048, 256)


def kernel(x, adj, L1_gnn_W_sa, L1_gnn_a_sa, L1_gnn_W_gcnb, L1_gnn_b_gcnb, L1_gnn_Wa, L1_gnn_ba, L1_gnn_Wb, L1_gnn_bb):
    import numpy as np
    import concourse.bacc as bacc
    from concourse import mybir as mb
    from concourse.bass_utils import run_bass_kernel_spmd

    x, adj = np.asarray(x), np.asarray(adj)
    w_sa, w_g = np.asarray(L1_gnn_W_sa), np.asarray(L1_gnn_W_gcnb)
    wa, wb = np.asarray(L1_gnn_Wa), np.asarray(L1_gnn_Wb)
    n, d = x.shape
    gap = np.zeros((d, 1), np.float32)
    adj_t = adj.reshape(n // 128, 128, n // 128, 128).transpose(0, 3, 2, 1).reshape(n // 128, 128, n)
    arrays = {
        "x": x,
        "adj": adj,
        "adj_t": adj_t,
        "w_cat": np.concatenate([w_sa, gap, gap, wa[:, d:].T, wb[:, d:].T, w_g, wa[:, :d].T, wb[:, :d].T], axis=1),
        "a_sa": np.asarray(L1_gnn_a_sa),
        "bias_row": np.concatenate([np.asarray(L1_gnn_b_gcnb), np.asarray(L1_gnn_ba), np.asarray(L1_gnn_bb)])[None],
    }
    arrays = {k: np.ascontiguousarray(v) for k, v in arrays.items()}
    nc = bacc.Bacc("TRN2", target_bir_lowering=False, num_devices=1)
    args = [nc.dram_tensor(k, v.shape, mb.dt.from_np(v.dtype), kind="ExternalInput").ap() for k, v in arrays.items()]
    args.append(nc.dram_tensor("out", _OUT, mb.dt.float32, kind="ExternalOutput").ap())
    two_layer_gnn(nc, *args)
    r = run_bass_kernel_spmd(nc, [arrays], core_ids=[0])
    return r.results[0]["out"]
```
